# Optimizing a Trainium2 kernel written in Bass

```python
import numpy as np
import jax
import jax.numpy as jnp

def _softmax(x, axis=-1):
    return jax.nn.softmax(x, axis=axis)

def _gelu(x):
    return jax.nn.gelu(x, approximate=True)

def _silu(x):
    return jax.nn.silu(x)

def _sigmoid(x):
    return jax.nn.sigmoid(x)

def _layernorm(x, axis=-1, eps=1e-05):
    m = jnp.mean(x, axis=axis, keepdims=True)
    v = jnp.var(x, axis=axis, keepdims=True)
    return (x - m) / jnp.sqrt(v + eps)

def _scatter_add(tgt, idx, src, axis=0):
    return tgt.at[idx].add(src)

def _segment_sum(src, seg, n):
    return jax.ops.segment_sum(src, seg, n)
kernel_name = 'mk_sandwich_d1_jaxref_r4_36eee2'

def setup_inputs(seed: int=0):
    np.random.seed(seed)
    _w = jnp.asarray

    def _L0_attn_setup():
        import math
        import jax, jax.numpy as jnp
        import numpy as np
        B, N, D_MODEL, H = (2, 1024, 512, 16)
        HEAD_DIM = D_MODEL // H
        CHUNK = 128

        def _slopes(n_heads):
            start = 2.0 ** (-2.0 ** (-(math.log2(n_heads) - 3)))
            return np.array([start ** (i + 1) for i in range(n_heads)], dtype=np.float32)

        def _lightning_attn(q, k, v):
            b, h, n, d = q.shape
            nc = n // CHUNK
            lam = jnp.exp(-jnp.asarray(_slopes(h)))
            pos = jnp.arange(CHUNK, dtype=jnp.float32)
            decay_q = lam[:, None] ** (pos + 1.0)
            decay_k = lam[:, None] ** (CHUNK - 1.0 - pos)
            diff = pos[:, None] - pos[None, :]
            causal = diff >= 0
            dmask = jnp.where(causal, lam[:, None, None] ** jnp.maximum(diff, 0.0), 0.0)
            lam_c = lam ** CHUNK

            def to_chunks(t):
                return t.reshape(b, h, nc, CHUNK, d).transpose(2, 0, 1, 3, 4)
            qc, kc, vc = (to_chunks(q), to_chunks(k), to_chunks(v))

            def step(S, inp):
                qb, kb, vb = inp
                inter = jnp.einsum('bhcd,bhde->bhce', qb * decay_q[None, :, :, None], S)
                scores = jnp.einsum('bhcd,bhed->bhce', qb, kb) * dmask[None]
                intra = jnp.einsum('bhce,bhed->bhcd', scores, vb)
                S_new = lam_c[None, :, None, None] * S + jnp.einsum('bhcd,bhce->bhde', kb * decay_k[None, :, :, None], vb)
                return (S_new, inter + intra)
            S0 = jnp.zeros((b, h, d, d), dtype=q.dtype)
            _, out = jax.lax.scan(step, S0, (qc, kc, vc))
            return out.transpose(1, 2, 0, 3, 4).reshape(b, h, n, d)
        key = jax.random.key(seed)
        kx, k1, k2, k3, k4 = jax.random.split(key, 5)
        scale = 1.0 / math.sqrt(D_MODEL)
        x = jax.random.normal(kx, (B, N, D_MODEL), dtype=jnp.float32)
        w_qkv = jax.random.normal(k1, (3 * D_MODEL, D_MODEL), dtype=jnp.float32) * scale
        b_qkv = jax.random.normal(k2, (3 * D_MODEL,), dtype=jnp.float32) * 0.01
        w_out = jax.random.normal(k3, (D_MODEL, D_MODEL), dtype=jnp.float32) * scale
        b_out = jax.random.normal(k4, (D_MODEL,), dtype=jnp.float32) * 0.01
        return {'x': x, 'w_qkv': w_qkv, 'b_qkv': b_qkv, 'w_out': w_out, 'b_out': b_out}
    _L0_attn_in = _L0_attn_setup()

    def _L0_ffn_setup():
        import jax, jax.numpy as jnp
        import numpy as np
        B, S, H, I = (1, 64, 512, 1536)

        def _quantized_matmul(x, w, scale):
            wq = w.astype(jnp.float8_e4m3fn).astype(x.dtype)
            y = jnp.einsum('bsi,io->bso', x, wq)
            return y * scale
        key = jax.random.key(seed)
        ks = jax.random.split(key, 7)
        return {'x': jax.random.normal(ks[0], (B, S, H), dtype=jnp.float32), 'gate_w': jax.random.normal(ks[1], (H, I), dtype=jnp.float32) * 0.02, 'up_w': jax.random.normal(ks[2], (H, I), dtype=jnp.float32) * 0.02, 'down_w': jax.random.normal(ks[3], (I, H), dtype=jnp.float32) * 0.02, 'gate_scale': jax.random.uniform(ks[4], (I,), dtype=jnp.float32, minval=0.5, maxval=1.5), 'up_scale': jax.random.uniform(ks[5], (I,), dtype=jnp.float32, minval=0.5, maxval=1.5), 'down_scale': jax.random.uniform(ks[6], (H,), dtype=jnp.float32, minval=0.5, maxval=1.5)}
    _L0_ffn_in = _L0_ffn_setup()
    _d = {'L0_attn_x': _L0_attn_in['x'], 'L0_attn_w_qkv': _L0_attn_in['w_qkv'], 'L0_attn_b_qkv': _L0_attn_in['b_qkv'], 'L0_attn_w_out': _L0_attn_in['w_out'], 'L0_attn_b_out': _L0_attn_in['b_out'], 'L0_ffn_gate_w': _L0_ffn_in['gate_w'], 'L0_ffn_up_w': _L0_ffn_in['up_w'], 'L0_ffn_down_w': _L0_ffn_in['down_w'], 'L0_ffn_gate_scale': _L0_ffn_in['gate_scale'], 'L0_ffn_up_scale': _L0_ffn_in['up_scale'], 'L0_ffn_down_scale': _L0_ffn_in['down_scale']}
    _x0 = _d['L0_attn_x']
    _d['L0_attn_x'] = jax.random.normal(jax.random.fold_in(jax.random.key(seed), 1), (4, 1024, 512), dtype=_x0.dtype)
    del _x0
    return _d

def reference(L0_attn_x, L0_attn_w_qkv, L0_attn_b_qkv, L0_attn_w_out, L0_attn_b_out, L0_ffn_gate_w, L0_ffn_up_w, L0_ffn_down_w, L0_ffn_gate_scale, L0_ffn_up_scale, L0_ffn_down_scale):

    def _L0_attn_ref(x, w_qkv, b_qkv, w_out, b_out):
        import math
        import jax, jax.numpy as jnp
        import numpy as np
        B, N, D_MODEL, H = (2, 1024, 512, 16)
        HEAD_DIM = D_MODEL // H
        CHUNK = 128

        def _slopes(n_heads):
            start = 2.0 ** (-2.0 ** (-(math.log2(n_heads) - 3)))
            return np.array([start ** (i + 1) for i in range(n_heads)], dtype=np.float32)

        def _lightning_attn(q, k, v):
            b, h, n, d = q.shape
            nc = n // CHUNK
            lam = jnp.exp(-jnp.asarray(_slopes(h)))
            pos = jnp.arange(CHUNK, dtype=jnp.float32)
            decay_q = lam[:, None] ** (pos + 1.0)
            decay_k = lam[:, None] ** (CHUNK - 1.0 - pos)
            diff = pos[:, None] - pos[None, :]
            causal = diff >= 0
            dmask = jnp.where(causal, lam[:, None, None] ** jnp.maximum(diff, 0.0), 0.0)
            lam_c = lam ** CHUNK

            def to_chunks(t):
                return t.reshape(b, h, nc, CHUNK, d).transpose(2, 0, 1, 3, 4)
            qc, kc, vc = (to_chunks(q), to_chunks(k), to_chunks(v))

            def step(S, inp):
                qb, kb, vb = inp
                inter = jnp.einsum('bhcd,bhde->bhce', qb * decay_q[None, :, :, None], S)
                scores = jnp.einsum('bhcd,bhed->bhce', qb, kb) * dmask[None]
                intra = jnp.einsum('bhce,bhed->bhcd', scores, vb)
                S_new = lam_c[None, :, None, None] * S + jnp.einsum('bhcd,bhce->bhde', kb * decay_k[None, :, :, None], vb)
                return (S_new, inter + intra)
            S0 = jnp.zeros((b, h, d, d), dtype=q.dtype)
            _, out = jax.lax.scan(step, S0, (qc, kc, vc))
            return out.transpose(1, 2, 0, 3, 4).reshape(b, h, n, d)
        b, n, dm = x.shape
        qkv = x @ w_qkv.T + b_qkv
        q, k, v = jnp.split(qkv, 3, axis=-1)

        def heads(t):
            return t.reshape(b, n, H, HEAD_DIM).transpose(0, 2, 1, 3)
        attn = _lightning_attn(heads(q), heads(k), heads(v))
        attn = attn.transpose(0, 2, 1, 3).reshape(b, n, dm)
        return attn @ w_out.T + b_out

    def _L0_ffn_ref(x, gate_w, up_w, down_w, gate_scale, up_scale, down_scale):
        import jax, jax.numpy as jnp
        import numpy as np
        B, S, H, I = (1, 64, 512, 1536)

        def _quantized_matmul(x, w, scale):
            wq = w.astype(jnp.float8_e4m3fn).astype(x.dtype)
            y = jnp.einsum('bsi,io->bso', x, wq)
            return y * scale
        gate = jax.nn.silu(_quantized_matmul(x, gate_w, gate_scale))
        up = _quantized_matmul(x, up_w, up_scale)
        fuse = gate * up
        return _quantized_matmul(fuse, down_w, down_scale)
    x = L0_attn_x
    x = x + _layernorm(_L0_attn_ref(_layernorm(x, axis=-1), L0_attn_w_qkv, L0_attn_b_qkv, L0_attn_w_out, L0_attn_b_out), axis=-1)
    x = x + _layernorm(_L0_ffn_ref(_layernorm(x, axis=-1), L0_ffn_gate_w, L0_ffn_up_w, L0_ffn_down_w, L0_ffn_gate_scale, L0_ffn_up_scale, L0_ffn_down_scale), axis=-1)
    return x

_drawn_inputs = setup_inputs


def setup_inputs(seed=0):
    import zlib

    import numpy as np

    out = dict(_drawn_inputs(seed))
    spreads = {}
    factors = {'L0_attn_b_qkv': 4.265, 'L0_attn_b_out': 200.0}
    for name, (base, spread) in spreads.items():
        noise = np.random.default_rng([zlib.crc32(name.encode()), seed]).standard_normal(out[name].shape)
        drawn = base * np.exp(spread * noise) if base else spread * noise
        out[name] = jnp.asarray(drawn.astype(out[name].dtype))
    for name, factor in factors.items():
        out[name] = (out[name] * factor).astype(out[name].dtype)
    return out
```

```python
from contextlib import ExitStack

import numpy as np

import concourse.bass as bass
from concourse import mybir

F32 = mybir.dt.float32
F16 = mybir.dt.float16
U32 = mybir.dt.uint32
ALU = mybir.AluOpType
ACT = mybir.ActivationFunctionType
AX = mybir.AxisListType
RMAX = bass.bass_isa.ReduceOp.max

P = 128
D = 512
KT = D // P
I = 1536
IT = I // P
H = 16
DH = D // H
HG = P // DH
TOK = 256
T = TOK // P
EPS = 1e-5
P_SHIFT = 20
EXPONENT = 0x7F800000
E4M3_TINY = 2.0 ** -6
E4M3_MAGIC = 1.5 * 2.0 ** 20
E4M3_NAN = float(np.float32(3.4028235e38 / 464.0))


def sandwich(nc, x, w_qkv_t, b_qk, b_v, w_out_t, b_out, gate_w, up_w, down_w, gate_s, up_s, down_s,
             mask_c, decay_q_c, decay_k_c, lam_c, eye_c, out):
    units = x.shape[0] // TOK
    per_seq = 1024 // TOK
    x_u = x.rearrange("(n t p) d -> n p t d", t=T, p=P)
    out_u = out.rearrange("(n t p) d -> n t p d", t=T, p=P)

    with ExitStack() as ctx:
        def sb(name, shape, dt=F32):
            return ctx.enter_context(nc.sbuf_tensor(name, shape, dt))

        def sem(name):
            return ctx.enter_context(nc.semaphore(name))

        wqkv_hi = sb("wqkv_hi", [P, KT, 3 * D], F16)
        wqkv_lo = sb("wqkv_lo", [P, KT, 3 * D], F16)
        wout = sb("wout", [P, KT, D])
        gate_q = sb("gate_q", [P, KT, I], F16)
        up_q = sb("up_q", [P, KT, I], F16)
        down_q = sb("down_q", [P, IT, D], F16)
        mask = sb("mask", [P, H, P])
        decay_q = sb("decay_q", [P, D])
        decay_k = sb("decay_k", [P, D])
        lam = sb("lam", [P, KT, P])
        eye = sb("eye", [P, P])
        bqk = sb("bqk", [P, 2 * KT])
        bv = sb("bv", [P, D])
        bo = sb("bo", [P, D])
        ds_t = sb("ds_t", [P, D])
        gs_t = sb("gs_t", [P, IT])
        us_t = sb("us_t", [P, IT])
        small = sb("small", [P, 48])
        eps_t = sb("eps_t", [P, 2, T])

        x_t = sb("x_t", [P, 2, T, D])
        nrm = sb("nrm", [P, T, D])
        x_hl = sb("x_hl", [P, 2, KT, TOK], F16)
        qk = sb("qk", [P, 2 * KT, TOK])
        v32 = sb("v32", [P, T, D])
        v_hl = sb("v_hl", [P, 2, T, D], F16)
        kd = sb("kd", [P, T, D])
        p32 = sb("p32", [P, 2, D])
        o32 = sb("o32", [P, T, D])
        o_t = sb("o_t", [P, T, KT, P])
        y32 = sb("y32", [P, T, D])
        state = sb("state", [P, KT, P])
        state_d = sb("state_d", [P, KT, P])
        x1 = sb("x1", [P, 2, T, D])
        stats = sb("stats", [P, 4, T, 6])
        mv = sb("mv", [P, 4, T, 2])
        rstd = sb("rstd", [P, 4, 2, T])

        att_pool = sb("att_pool", [P, KT * 3 * D])
        stacks = att_pool[:, 0:2 * H * TOK // 2].bitcast(F16).rearrange(
            "p (s h t) -> p s h t", s=2, h=H)
        split = att_pool[:, 2 * H * TOK // 2:KT * 3 * D].bitcast(F16)
        qk_hl = split.rearrange("p (s k t) -> p s k t", s=2, k=2 * KT)
        pr_hl = split.rearrange("p (s h c) -> p s h c", s=2, h=H)
        w_stage = att_pool[:, :].rearrange("p (k n) -> p k n", k=KT)
        ffn_pool = sb("ffn_pool", [P, 6656])
        h_hl = ffn_pool[:, 0:3072].bitcast(F16).rearrange("p (s k t) -> p s k t", s=2, k=IT)
        sil = ffn_pool[:, 3072:3584].rearrange("p (j t) -> p j t", j=2)
        y2 = ffn_pool[:, 3584:4608].rearrange("p (t d) -> p t d", t=T)
        h32 = ffn_pool[:, 4608:5632].rearrange("p (i n) -> p i n", i=2)
        x1_hl = ffn_pool[:, 5632:6656].bitcast(F16).rearrange("p (s k t) -> p s k t", s=2, k=KT)
        f_stage = [ffn_pool[:, 0:1536], ffn_pool[:, 1536:3072]]
        f_magic = [ffn_pool[:, 3072:4608], ffn_pool[:, 4608:6144]]

        bank = [ctx.enter_context(nc.psum_tensor(f"bank{n}", [P, D], F32)) for n in range(8)]
        b_gate, b_up, b_y, b_att = bank[0], bank[1], bank[2], bank[7]
        b_t = [bank[3], bank[4]]
        b_s = [bank[5], bank[6]]

        w_in = [sem(f"w_in{k}") for k in range(KT)]
        bias_in, tab_in, scl_in, wout_in = sem("bias_in"), sem("tab_in"), sem("scl_in"), sem("wout_in")
        f_in = [sem("f_in0"), sem("f_in1")]
        chain = sem("chain")
        w_max, w_max_all = sem("w_max"), sem("w_max_all")
        w_hi_d, w_lo_d = sem("w_hi_d"), sem("w_lo_d")
        f_magic_d, f_sum_d, f_q_d = sem("f_magic_d"), sem("f_sum_d"), sem("f_q_d")
        f_max, f_max_all, f_scale_d = sem("f_max"), sem("f_max_all"), sem("f_scale_d")
        bn_seen = sem("bn_seen")
        state_0, eps_d = sem("state_0"), sem("eps_d")
        x_in = [sem("x_in0"), sem("x_in1")]
        y2_free = sem("y2_free")
        q_stacked, k_stacked, stored = sem("q_stacked"), sem("k_stacked"), sem("stored")
        x_tr, qk_mm, v_mm, x1_tr, k_tr = sem("x_tr"), sem("qk_mm"), sem("v_mm"), sem("x1_tr"), sem("k_tr")
        score_mm, carry_mm, state_mm, att_mm = sem("score_mm"), sem("carry_mm"), sem("state_mm"), sem("att_mm")
        o_tr, out_mm, gate_mm, up_mm, down_mm = sem("o_tr"), sem("out_mm"), sem("gate_mm"), sem("up_mm"), sem("down_mm")
        x_hi_d, qk_d, qk_hi_d, v_hi_d, x1_hi_d = sem("x_hi_d"), sem("qk_d"), sem("qk_hi_d"), sem("v_hi_d"), sem("x1_hi_d")
        p_hi_d, o_t_d, silu_d, h_hi_d = sem("p_hi_d"), sem("o_t_d"), sem("silu_d"), sem("h_hi_d")
        x_lo_d, v_d, kd_d, x1_lo_d = sem("x_lo_d"), sem("v_d"), sem("kd_d"), sem("x1_lo_d")
        p_d, carry_d, state_u, o_d, h_d, y_d, y2_d = (sem("p_d"), sem("carry_d"), sem("state_u"), sem("o_d"),
                                                      sem("h_d"), sem("y_d"), sem("y2_d"))
        bn_d = [sem(f"bn_d{n}") for n in range(4)]
        mv_d = [sem(f"mv_d{n}") for n in range(4)]
        nrm_d = [sem(f"nrm_d{n}") for n in range(4)]
        qk_lo_d, v_lo_d, p_lo_d, h_lo_d = sem("qk_lo_d"), sem("v_lo_d"), sem("p_lo_d"), sem("h_lo_d")
        state_dec, x1_d, fin_d = sem("state_dec"), sem("x1_d"), sem("fin_d")
        ve_d = [sem(f"ve_d{n}") for n in range(4)]
        rs_d = [sem(f"rs_d{n}") for n in range(4)]

        N_BIAS, N_TAB, N_SCL = 2, 5, 3
        LN_X, LN_Y, LN_X1, LN_Y2 = range(4)
        last = units - 1

        def piece_in(n):
            w, k = (gate_w, up_w, down_w)[n // 4], n % 4
            if n < 8:
                return w[k * P:(k + 1) * P, :]
            return w[3 * k * P:3 * (k + 1) * P, :].rearrange("(c p) n -> p c n", p=P)

        def stage_for(n):
            return f_stage[n % 2] if n < 8 else f_stage[n % 2].rearrange("p (c n) -> p c n", n=D)

        def piece_out(n):
            if n < 8:
                return (gate_q, up_q)[n // 4][:, n % 4]
            return down_q[:, 3 * (n % 4):3 * (n % 4) + 3].rearrange("p c n -> p (c n)")

        def slots(fori, slot, start, end):
            start()
            slot(0, 0, att=True, ffn=False, nxt=True)
            with fori(0, (units - per_seq) // per_seq) as seq:
                for j in range(1, per_seq + 1):
                    slot(seq * per_seq + j, j % per_seq, att=True, ffn=True, nxt=True)
            for s in range(units - per_seq + 1, units + 1):
                slot(s, s % per_seq, att=s < units, ffn=True, nxt=s < last)
            end()

        block = ctx.enter_context(nc.Block())

        @block.sync
        def _(sp):
            def start():
                sp.sem_inc(y2_free, 1)
                sp.dma_start(x_t[:, 0], x_u[0]).then_inc(x_in[0], 16)
                for k in range(KT):
                    sp.dma_start(w_stage[:, k], w_qkv_t[k * P:(k + 1) * P, :]).then_inc(w_in[k], 16)
                sp.dma_start(bv[:, :], b_v).then_inc(bias_in, 16)
                for dst, src in ((mask[:, :, :], mask_c), (decay_q[:, :], decay_q_c),
                                 (decay_k[:, :], decay_k_c), (lam[:, :, :], lam_c)):
                    sp.dma_start(dst, src).then_inc(tab_in, 16)
                sp.dma_start(wout[:, :, :], w_out_t.rearrange("(k p) n -> p k n", p=P)).then_inc(wout_in, 16)
                sp.dma_start(bo[:, :], b_out).then_inc(wout_in, 16)

            def stack(n):
                for which, done, parts in ((0, q_stacked, (0, 1, 0, 1)), (1, k_stacked, (0, 0, 1, 1))):
                    sp.wait_ge(qk_hi_d, 4 * n + 2 + 2 * which)
                    sp.wait_ge(qk_lo_d, 4 * n + 2 + 2 * which)
                    for j in range(HG):
                        for r in range(4):
                            sp.dma_start(stacks[DH * r:DH * (r + 1), which, j::HG, :],
                                         qk_hl[DH * j:DH * (j + 1), parts[r], KT * which:KT * (which + 1), :]
                                         ).then_inc(done, 16)

            def slot(s, m, att, ffn, nxt):
                if nxt:
                    if not (type(s) is int and s == 0):
                        sp.wait_ge(x1_d, 2 * s)
                    sp.dma_start(x_t[:, (m + 1) % 2], x_u[s + 1]).then_inc(x_in[(m + 1) % 2], 16)
                if not ffn:
                    stack(0)
                    for n in range(2, 12):
                        sp.wait_ge(f_q_d, n - 1)
                        sp.dma_start(stage_for(n), piece_in(n)).then_inc(f_in[n % 2], 16)
                if nxt:
                    stack(s + 1)
                if ffn:
                    for t in range(T):
                        sp.wait_ge(fin_d, 2 * (s - 1) + t + 1)
                        sp.dma_start(out_u[s - 1, t], y2[:, t]).then_inc(stored, 16)
                    sp.wait_ge(stored, 16 * T * s)
                    sp.sem_inc(y2_free, 1)

            slots(sp.Fori, slot, start, lambda: None)

        @block.scalar
        def _(act):
            def start():
                act.dma_start(eye[:, :], eye_c).then_inc(tab_in, 16)
                act.dma_start(bqk[:, :], b_qk).then_inc(bias_in, 16)
                act.dma_start(gs_t[:, :], gate_s).then_inc(scl_in, 16)
                act.dma_start(us_t[:, :], up_s).then_inc(scl_in, 16)
                act.dma_start(ds_t[:, :], down_s).then_inc(scl_in, 16)
                for n in range(2):
                    act.dma_start(stage_for(n), piece_in(n)).then_inc(f_in[n], 16)
                split_x(0)
                front(0)
                v_hi(0)

            def front(n):
                for i in range(4):
                    act.wait_ge(qk_mm, 4 * n + i + 1)
                    for j in range(2):
                        o = 2 * i + j
                        ins = nc.scalar.activation(qk[:, o], b_t[i % 2][:, j * TOK:(j + 1) * TOK],
                                                   ACT.Identity, bias=bqk[:, o:o + 1])
                    ins.then_inc(qk_d, 1)
                    act.wait_ge(qk_d, 4 * n + i + 1)
                    nc.scalar.copy(qk_hl[:, 0, 2 * i:2 * i + 2].rearrange("p k t -> p (k t)"),
                                   qk[:, 2 * i:2 * i + 2].rearrange("p k t -> p (k t)")).then_inc(qk_hi_d, 1)

            def v_hi(n):
                for t in range(T):
                    act.wait_ge(v_d, 2 * n + t + 1)
                    nc.scalar.copy(v_hl[:, 0, t], v32[:, t]).then_inc(v_hi_d, 1)

            def split_x(n):
                for j in range(2):
                    act.wait_ge(x_tr, 2 * n + j + 1)
                    nc.scalar.copy(x_hl[:, 0, 2 * j:2 * j + 2].rearrange("p k t -> p (k t)"),
                                   b_s[j][:, :]).then_inc(x_hi_d, 1)

            def probs_hi(s, c):
                if c:
                    act.wait_ge(att_mm, 2 * s + 1)
                for g in range(KT):
                    act.wait_ge(p_d, 8 * s + 4 * c + g + 1)
                    nc.scalar.copy(pr_hl[:, 0, 4 * g:4 * g + 4].rearrange("p h c -> p (h c)"),
                                   p32[:, g % 2]).then_inc(p_hi_d, 1)

            def silu(v, i):
                act.wait_ge(gate_mm, 6 * v + i + 1)
                if i:
                    act.wait_ge(h_d, 6 * v + i)
                for j in range(2):
                    ins = nc.scalar.activation(sil[:, j], b_gate[:, j * TOK:(j + 1) * TOK], ACT.Silu,
                                               scale=gs_t[:, 2 * i + j:2 * i + j + 1])
                ins.then_inc(silu_d, 1)

            def h_hi(v, i):
                act.wait_ge(h_d, 6 * v + i + 1)
                nc.scalar.copy(h_hl[:, 0, 2 * i:2 * i + 2].rearrange("p k t -> p (k t)"),
                               h32[:, i % 2]).then_inc(h_hi_d, 1)

            def out_t(s, c):
                act.wait_ge(o_tr, 2 * s + c + 1)
                nc.scalar.copy(o_t[:, c].rearrange("p k c -> p (k c)"), b_s[c][:, :]).then_inc(o_t_d, 1)

            def slot(s, m, att, ffn, nxt):
                v = s - 1
                if ffn:
                    for j in range(2):
                        act.wait_ge(x1_tr, 2 * v + j + 1)
                        nc.scalar.copy(x1_hl[:, 0, 2 * j:2 * j + 2].rearrange("p k t -> p (k t)"),
                                       (b_y, b_att)[j][:, :]).then_inc(x1_hi_d, 1)
                if att:
                    probs_hi(s, 0)
                if ffn:
                    if type(s) is int and s == 1:
                        act.wait_ge(f_scale_d, 1)
                    silu(v, 0)
                    silu(v, 1)
                    h_hi(v, 0)
                    silu(v, 2)
                    h_hi(v, 1)
                if att:
                    probs_hi(s, 1)
                if ffn:
                    silu(v, 3)
                    h_hi(v, 2)
                if nxt:
                    split_x(s + 1)
                if ffn:
                    silu(v, 4)
                    h_hi(v, 3)
                    silu(v, 5)
                    h_hi(v, 4)
                    h_hi(v, 5)
                if att:
                    out_t(s, 0)
                if nxt:
                    front(s + 1)
                if att:
                    out_t(s, 1)
                if nxt:
                    v_hi(s + 1)

            slots(act.Fori, slot, start, lambda: None)

        @block.tensor
        def _(pe):
            def transpose_x(n):
                pe.wait_ge(nrm_d[LN_X], 2 * n + 2)
                for j in range(2):
                    for kk in range(2):
                        for t in range(T):
                            ins = nc.tensor.transpose(b_s[j][:, kk * TOK + t * P:kk * TOK + (t + 1) * P],
                                                      nrm[:, t, (2 * j + kk) * P:(2 * j + kk + 1) * P], eye[:, :])
                    ins.then_inc(x_tr, 1)

            def start():
                pe.wait_ge(tab_in, 16 * N_TAB)
                transpose_x(0)
                project_qk(0)
                project_v(0)
                transpose_k(0)
                pe.wait_ge(state_0, 1)

            def gate_up(v, i):
                if i == 0:
                    pe.wait_ge(x1_lo_d, 2 * v + 2)
                else:
                    pe.wait_ge(silu_d, 6 * v + i)
                for w, b, done in ((gate_q, b_gate, gate_mm), (up_q, b_up, up_mm)):
                    if done is up_mm and i:
                        pe.wait_ge(h_d, 6 * v + i)
                    for j in range(2):
                        o = 2 * i + j
                        for k in range(KT):
                            for part in range(2):
                                ins = nc.tensor.matmul(b[:, j * TOK:(j + 1) * TOK], w[:, k, o * P:(o + 1) * P],
                                                       x1_hl[:, part, k], start=(k == 0 and part == 0),
                                                       stop=(k == KT - 1 and part == 1))
                    ins.then_inc(done, 1)

            def down(v, t):
                pe.wait_ge(h_hi_d, 6 * v + 6)
                pe.wait_ge(h_lo_d, 6 * v + 6)
                for k in range(IT):
                    for part in range(2):
                        ins = nc.tensor.matmul((b_gate, b_up)[t][:, :], h_hl[:, part, k, t * P:(t + 1) * P],
                                               down_q[:, k], start=(k == 0 and part == 0),
                                               stop=(k == IT - 1 and part == 1))
                ins.then_inc(down_mm, 1)

            def scores(s, c):
                if c == 0:
                    pe.wait_ge(q_stacked, 256 * s + 256)
                    pe.wait_ge(k_stacked, 256 * s + 256)
                    if not (type(s) is int and s == 0):
                        pe.wait_ge(o_t_d, 2 * s)
                for g in range(KT):
                    if c or g >= 2:
                        pe.wait_ge(p_d, 8 * s + 4 * c + g - 1)
                    for j in range(HG):
                        h = HG * g + j
                        ins = nc.tensor.matmul(b_s[g % 2][:, j * P:(j + 1) * P],
                                               stacks[:, 1, h, c * P:(c + 1) * P],
                                               stacks[:, 0, h, c * P:(c + 1) * P], start=True, stop=True)
                    ins.then_inc(score_mm, 1)

            def carry_and_state(s, c):
                if c == 0:
                    pe.wait_ge(kd_d, 2 * s + 2)
                else:
                    pe.wait_ge(carry_d, 2 * s + 1)
                if not (c == 0 and type(s) is int and s == 0):
                    pe.wait_ge(state_u, 2 * s + c)
                for g in range(KT):
                    ins = nc.tensor.matmul(b_t[0][:, g * P:(g + 1) * P], qk[:, g, c * P:(c + 1) * P],
                                           state[:, g], start=True, stop=True)
                ins.then_inc(carry_mm, 1)
                for g in range(KT):
                    ins = nc.tensor.matmul(b_t[1][:, g * P:(g + 1) * P], kd[:, c, g * P:(g + 1) * P],
                                           v32[:, c, g * P:(g + 1) * P], start=True, stop=True)
                ins.then_inc(state_mm, 1)

            def attend(s, c):
                pe.wait_ge(p_hi_d, 8 * s + 4 * c + 4)
                pe.wait_ge(p_lo_d, 8 * s + 4 * c + 4)
                pe.wait_ge(v_hi_d, 2 * s + c + 1)
                pe.wait_ge(v_lo_d, 2 * s + c + 1)
                if c:
                    pe.wait_ge(o_d, 2 * s + 1)
                for h in range(H):
                    for n, (a, b) in enumerate(((0, 0), (0, 1), (1, 0))):
                        ins = nc.tensor.matmul(b_att[:, h * DH:(h + 1) * DH], pr_hl[:, a, h],
                                               v_hl[:, b, c, h * DH:(h + 1) * DH], start=(n == 0), stop=(n == 2))
                ins.then_inc(att_mm, 1)

            def transpose_o(s, c, nxt):
                pe.wait_ge(o_d, 2 * s + c + 1)
                if nxt:
                    pe.wait_ge(x_lo_d, 2 * s + 4)
                elif c == 0:
                    pe.wait_ge(p_d, 8 * s + 8)
                for k in range(KT):
                    ins = nc.tensor.transpose(b_s[c][:, k * P:(k + 1) * P], o32[:, c, k * P:(k + 1) * P], eye[:, :])
                ins.then_inc(o_tr, 1)

            def project(s, c):
                pe.wait_ge(o_t_d, 2 * s + c + 1)
                for k in range(KT):
                    ins = nc.tensor.matmul((b_y, b_att)[c][:, :], o_t[:, c, k], wout[:, k], start=(k == 0),
                                           stop=(k == KT - 1))
                ins.then_inc(out_mm, 1)

            def project_qk(n):
                first = type(n) is int and n == 0
                pe.wait_ge(x_lo_d, 2 * n + 2)
                for i in range(4):
                    if i >= 2:
                        pe.wait_ge(qk_d, 4 * n + i - 1)
                    elif not first:
                        pe.wait_ge((carry_d, state_u)[i], 2 * n)
                    for j in range(2):
                        o = 2 * i + j
                        for k in range(KT):
                            if first and i == 0 and j == 0:
                                pe.wait_ge(w_hi_d, k + 1)
                                pe.wait_ge(w_lo_d, k + 1)
                            for q, (a, b) in enumerate(((0, 0), (0, 1), (1, 0))):
                                ins = nc.tensor.matmul(b_t[i % 2][:, j * TOK:(j + 1) * TOK],
                                                       (wqkv_hi, wqkv_lo)[a][:, k, o * P:(o + 1) * P],
                                                       x_hl[:, b, k], start=(k == 0 and q == 0),
                                                       stop=(k == KT - 1 and q == 2))
                    ins.then_inc(qk_mm, 1)

            def project_v(n):
                for t in range(T):
                    pe.wait_ge(qk_d, 4 * n + 3 + t)
                    for k in range(KT):
                        for q, (a, b) in enumerate(((0, 0), (0, 1), (1, 0))):
                            ins = nc.tensor.matmul(b_t[t][:, :], x_hl[:, b, k, t * P:(t + 1) * P],
                                                   (wqkv_hi, wqkv_lo)[a][:, k, 2 * D:3 * D],
                                                   start=(k == 0 and q == 0), stop=(k == KT - 1 and q == 2))
                    ins.then_inc(v_mm, 1)

            def transpose_k(n):
                for c in range(T):
                    pe.wait_ge(v_d, 2 * n + c + 1)
                    for g in range(KT):
                        ins = nc.tensor.transpose(b_t[c][:, g * P:(g + 1) * P],
                                                  qk[:, KT + g, c * P:(c + 1) * P], eye[:, :])
                    ins.then_inc(k_tr, 1)

            def slot(s, m, att, ffn, nxt):
                v = s - 1
                if ffn:
                    pe.wait_ge(nrm_d[LN_X1], 2 * v + 2)
                    for j in range(2):
                        for kk in range(2):
                            for t in range(T):
                                ins = nc.tensor.transpose((b_y, b_att)[j][:, kk * TOK + t * P:kk * TOK + (t + 1) * P],
                                                          nrm[:, t, (2 * j + kk) * P:(2 * j + kk + 1) * P], eye[:, :])
                        ins.then_inc(x1_tr, 1)
                if att:
                    scores(s, 0)
                if ffn:
                    gate_up(v, 0)
                    gate_up(v, 1)
                if att:
                    carry_and_state(s, 0)
                if ffn:
                    gate_up(v, 2)
                if att:
                    attend(s, 0)
                    scores(s, 1)
                if ffn:
                    gate_up(v, 3)
                if att:
                    carry_and_state(s, 1)
                if nxt:
                    pe.wait_ge(p_d, 8 * s + 8)
                    transpose_x(s + 1)
                if ffn:
                    gate_up(v, 4)
                if att:
                    attend(s, 1)
                if ffn:
                    gate_up(v, 5)
                if att:
                    transpose_o(s, 0, nxt)
                if nxt:
                    project_qk(s + 1)
                if att:
                    if type(s) is int and s == 0:
                        pe.wait_ge(wout_in, 32)
                    project(s, 0)
                if ffn:
                    down(v, 0)
                if att:
                    transpose_o(s, 1, nxt)
                    project(s, 1)
                if nxt:
                    project_v(s + 1)
                    transpose_k(s + 1)
                if ffn:
                    down(v, 1)

            slots(pe.Fori, slot, start, lambda: None)

        @block.gpsimd
        def _(pool):
            def inverse_std(ln, val, cols):
                nc.gpsimd.tensor_tensor(rstd[:, ln, 0, cols], mv[:, ln, cols, 1], eps_t[:, 0, cols],
                                        ALU.add).then_inc(ve_d[ln], 1)
                pool.wait_ge(ve_d[ln], val)
                nc.gpsimd.tensor_tensor(rstd[:, ln, 1, cols], rstd[:, ln, 0, cols], eps_t[:, 1, cols],
                                        ALU.pow).then_inc(rs_d[ln], 1)

            def inverse_std_x(n):
                pool.wait_ge(mv_d[LN_X], 2 * n + 2)
                inverse_std(LN_X, n + 1, slice(0, T))

            def start():
                nc.gpsimd.memset(eps_t[:, 0, :], EPS).then_inc(eps_d, 1)
                nc.gpsimd.memset(eps_t[:, 1, :], -0.5).then_inc(eps_d, 1)
                nc.gpsimd.memset(state[:, :, :], 0.0).then_inc(state_0, 1)
                pool.wait_ge(eps_d, 2)
                inverse_std_x(0)
                pool.wait_ge(w_max, 1)
                nc.gpsimd.partition_all_reduce(small[:, 6:7], small[:, 5:6], P, RMAX).then_inc(w_max_all, 1)
                pool.wait_ge(state_0, 1)
                qk_lo(0)
                v_lo(0)

            def quant_sum(n):
                pool.wait_ge(f_magic_d, n + 1)
                nc.gpsimd.tensor_tensor(f_stage[n % 2], f_stage[n % 2], f_magic[n % 2], ALU.add
                                        ).then_inc(f_sum_d, 1)

            def h_lo(v, i):
                pool.wait_ge(h_hi_d, 6 * v + i + 1)
                nc.gpsimd.tensor_tensor(h_hl[:, 1, 2 * i:2 * i + 2].rearrange("p k t -> p (k t)"), h32[:, i % 2],
                                        h_hl[:, 0, 2 * i:2 * i + 2].rearrange("p k t -> p (k t)"),
                                        ALU.subtract).then_inc(h_lo_d, 1)

            def state_decay(s, c):
                if not (c == 0 and type(s) is int and s == 0):
                    pool.wait_ge(state_u, 2 * s + c)
                nc.gpsimd.tensor_tensor(state_d[:, :, :], state[:, :, :], lam[:, :, :], ALU.mult
                                        ).then_inc(state_dec, 1)

            def probs_lo(s, c):
                for g in range(KT):
                    pool.wait_ge(p_hi_d, 8 * s + 4 * c + g + 1)
                    nc.gpsimd.tensor_tensor(pr_hl[:, 1, 4 * g:4 * g + 4].rearrange("p h c -> p (h c)"), p32[:, g % 2],
                                            pr_hl[:, 0, 4 * g:4 * g + 4].rearrange("p h c -> p (h c)"),
                                            ALU.subtract).then_inc(p_lo_d, 1)

            def qk_lo(n):
                for i in range(4):
                    pool.wait_ge(qk_hi_d, 4 * n + i + 1)
                    nc.gpsimd.tensor_tensor(qk_hl[:, 1, 2 * i:2 * i + 2].rearrange("p k t -> p (k t)"),
                                            qk[:, 2 * i:2 * i + 2].rearrange("p k t -> p (k t)"),
                                            qk_hl[:, 0, 2 * i:2 * i + 2].rearrange("p k t -> p (k t)"),
                                            ALU.subtract).then_inc(qk_lo_d, 1)

            def v_lo(n):
                for t in range(T):
                    pool.wait_ge(v_hi_d, 2 * n + t + 1)
                    nc.gpsimd.tensor_tensor(v_hl[:, 1, t], v32[:, t], v_hl[:, 0, t], ALU.subtract
                                            ).then_inc(v_lo_d, 1)

            def slot(s, m, att, ffn, nxt):
                v = s - 1
                if att:
                    if not ffn:
                        pool.wait_ge(tab_in, 16 * N_TAB)
                    probs_lo(s, 0)
                    state_decay(s, 0)
                if ffn:
                    for i in range(2):
                        h_lo(v, i)
                else:
                    for n in range(4):
                        quant_sum(n)
                if nxt:
                    inverse_std_x(s + 1)
                if att:
                    state_decay(s, 1)
                    probs_lo(s, 1)
                if ffn:
                    for i in range(2, 6):
                        h_lo(v, i)
                else:
                    for n in range(4, 8):
                        quant_sum(n)
                if nxt:
                    qk_lo(s + 1)
                if not ffn:
                    for n in range(8, 12):
                        quant_sum(n)
                for t in range(T):
                    if att:
                        pool.wait_ge(mv_d[LN_Y], 2 * s + t + 1)
                        inverse_std(LN_Y, 2 * s + t + 1, slice(t, t + 1))
                        pool.wait_ge(nrm_d[LN_Y], 2 * s + t + 1)
                        nc.gpsimd.tensor_tensor(x1[:, m % 2, t], x_t[:, m % 2, t], y32[:, t], ALU.add
                                                ).then_inc(x1_d, 1)
                        pool.wait_ge(mv_d[LN_X1], 2 * s + t + 1)
                        inverse_std(LN_X1, 2 * s + t + 1, slice(t, t + 1))
                    if nxt and t:
                        v_lo(s + 1)
                    if ffn:
                        pool.wait_ge(mv_d[LN_Y2], 2 * v + t + 1)
                        inverse_std(LN_Y2, 2 * v + t + 1, slice(t, t + 1))
                        pool.wait_ge(nrm_d[LN_Y2], 2 * v + t + 1)
                        nc.gpsimd.tensor_tensor(y2[:, t], x1[:, (m + 1) % 2, t], y2[:, t], ALU.add
                                                ).then_inc(fin_d, 1)
                if not ffn:
                    pool.wait_ge(f_max, 1)
                    nc.gpsimd.partition_all_reduce(small[:, 24:28], small[:, 20:24], P, RMAX).then_inc(f_max_all, 1)

            slots(pool.Fori, slot, start, lambda: None)

        @block.vector
        def _(dve):
            links = [0]

            def link(ins):
                links[0] += 1
                ins.then_inc(chain, 1)
                dve.wait_ge(chain, links[0])

            def col(a, n=1):
                return small[:, a:a + n]

            def power_of_two(dst, src, low, high):
                link(nc.vector.tensor_scalar(dst.bitcast(U32), src.bitcast(U32), EXPONENT, None, ALU.bitwise_and))
                link(nc.vector.tensor_scalar(dst, dst, low, high, ALU.max, ALU.min))

            def prepare_qkv():
                for k in range(KT):
                    dve.wait_ge(w_in[k], 16)
                    nc.vector.tensor_reduce(col(k), w_stage[:, k], AX.X, ALU.max, apply_absolute_value=True)
                dve.wait_ge(bias_in, 16 * N_BIAS)
                nc.vector.tensor_reduce(col(7), bqk[:, :], AX.X, ALU.max, apply_absolute_value=True)
                link(nc.vector.tensor_reduce(col(8), bv[:, :], AX.X, ALU.max, apply_absolute_value=True))
                link(nc.vector.tensor_tensor(col(7), col(7), col(8), ALU.max))
                link(nc.vector.tensor_scalar(col(4), col(7), 1.0 / 256.0, None, ALU.mult))
                nc.vector.tensor_reduce(col(5), col(0, 5), AX.X, ALU.max).then_inc(w_max, 1)
                dve.wait_ge(w_max_all, 1)
                power_of_two(col(9), col(6), 2.0 ** -30, 2.0 ** 35)
                link(nc.vector.tensor_scalar(col(10), col(9), 2.0 ** -5, None, ALU.mult))
                link(nc.vector.reciprocal(col(11), col(10)))
                for k in range(KT):
                    nc.vector.tensor_scalar(wqkv_hi[:, k], w_stage[:, k], col(11), None, ALU.mult).then_inc(w_hi_d, 1)
                    dve.wait_ge(w_hi_d, k + 1)
                    nc.vector.scalar_tensor_tensor(out=wqkv_lo[:, k], in0=w_stage[:, k], scalar=col(11),
                                                   in1=wqkv_hi[:, k], op0=ALU.mult, op1=ALU.subtract
                                                   ).then_inc(w_lo_d, 1)
                nc.vector.tensor_scalar(bqk[:, :], bqk[:, :], col(11), None, ALU.mult)
                nc.vector.tensor_scalar(bv[:, :], bv[:, :], col(11), None, ALU.mult)
                link(nc.vector.tensor_tensor(col(12), col(10), col(10), ALU.mult))
                link(nc.vector.scalar_tensor_tensor(out=col(13), in0=col(12), scalar=2.0 ** P_SHIFT, in1=col(10),
                                                    op0=ALU.mult, op1=ALU.mult))

            def quant(n):
                w, magic, q = f_stage[n % 2], f_magic[n % 2], piece_out(n)
                dve.wait_ge(f_in[n % 2], 16 * (n // 2 + 1))
                link(nc.vector.tensor_scalar(magic.bitcast(U32), w.bitcast(U32), EXPONENT, None, ALU.bitwise_and))
                nc.vector.tensor_scalar(magic, magic, E4M3_TINY, E4M3_MAGIC, ALU.max, ALU.mult
                                        ).then_inc(f_magic_d, 1)
                if n:
                    quant_end(n - 1)

            def quant_end(n):
                w, magic, q = f_stage[n % 2], f_magic[n % 2], piece_out(n)
                dve.wait_ge(f_sum_d, n + 1)
                link(nc.vector.tensor_tensor(q, w, magic, ALU.subtract))
                nan = magic.bitcast(F16)[:, 0:I]
                link(nc.vector.tensor_scalar(nan, q, E4M3_NAN, 0.0, ALU.mult, ALU.mult))
                nc.vector.tensor_tensor(q, q, nan, ALU.add).then_inc(f_q_d, 1)
                if n < 8:
                    dve.wait_ge(f_q_d, n + 1)
                    link(nc.vector.tensor_reduce(col(28 + n), q, AX.X, ALU.max, apply_absolute_value=True))

            def scale_h():
                dve.wait_ge(scl_in, 16 * N_SCL)
                nc.vector.tensor_reduce(col(20), col(28, 4), AX.X, ALU.max)
                nc.vector.tensor_reduce(col(21), col(32, 4), AX.X, ALU.max)
                nc.vector.tensor_reduce(col(22), gs_t[:, :], AX.X, ALU.max, apply_absolute_value=True)
                nc.vector.tensor_reduce(col(23), us_t[:, :], AX.X, ALU.max, apply_absolute_value=True
                                        ).then_inc(f_max, 1)
                dve.wait_ge(f_max_all, 1)
                link(nc.vector.tensor_tensor(col(36), col(24), col(25), ALU.mult))
                link(nc.vector.tensor_tensor(col(37), col(26), col(27), ALU.mult))
                link(nc.vector.scalar_tensor_tensor(out=col(38), in0=col(36), scalar=float(D * D), in1=col(37),
                                                    op0=ALU.mult, op1=ALU.mult))
                power_of_two(col(39), col(38), 2.0 ** -60, 2.0 ** 100)
                link(nc.vector.tensor_scalar(col(40), col(39), 2.0 ** -14, None, ALU.mult))
                link(nc.vector.reciprocal(col(41), col(40)))
                nc.vector.tensor_scalar(us_t[:, :], us_t[:, :], col(41), None, ALU.mult)
                link(nc.vector.tensor_scalar(ds_t[:, :], ds_t[:, :], col(40), None, ALU.mult))

            def moments(ln, val, src, t):
                nc.vector.bn_stats(stats[:, ln, t], src).then_inc(bn_d[ln], 1)
                dve.wait_ge(bn_d[ln], val)
                dve.sem_inc(bn_seen, 1)
                nc.vector.bn_aggr(mv[:, ln, t], stats[:, ln, t]).then_inc(mv_d[ln], 1)

            def normalise(ln, dst, src, t):
                nc.vector.tensor_scalar(dst, src, mv[:, ln, t, 0:1], rstd[:, ln, 1, t:t + 1], ALU.subtract,
                                        ALU.mult).then_inc(nrm_d[ln], 1)

            def moments_x(n, par):
                dve.wait_ge(x_in[par], 8 * (n - par) + 16)
                for t in range(T):
                    moments(LN_X, 2 * n + t + 1, x_t[:, par, t], t)

            def normalise_x(n, par):
                dve.wait_ge(rs_d[LN_X], n + 1)
                for t in range(T):
                    normalise(LN_X, nrm[:, t], x_t[:, par, t], t)

            def x_lo(n):
                for j in range(2):
                    dve.wait_ge(x_hi_d, 2 * n + j + 1)
                    nc.vector.tensor_tensor(x_hl[:, 1, 2 * j:2 * j + 2].rearrange("p k t -> p (k t)"), b_s[j][:, :],
                                            x_hl[:, 0, 2 * j:2 * j + 2].rearrange("p k t -> p (k t)"),
                                            ALU.subtract).then_inc(x_lo_d, 1)

            def start():
                moments_x(0, 0)
                normalise_x(0, 0)
                prepare_qkv()
                x_lo(0)
                dve.wait_ge(tab_in, 16 * N_TAB)
                for t in range(T):
                    v_sum(0, t)
                for c in range(T):
                    k_decay(0, c)

            def masked(s, c):
                for g in range(KT):
                    dve.wait_ge(score_mm, 8 * s + 4 * c + g + 1)
                    if not (type(s) is int and s == 0 and c == 0 and g < 2):
                        dve.wait_ge(p_lo_d, 8 * s + 4 * c + g - 1)
                    nc.vector.tensor_tensor(p32[:, g % 2], b_s[g % 2][:, :],
                                            mask[:, HG * g:HG * (g + 1)].rearrange("p h c -> p (h c)"),
                                            ALU.mult).then_inc(p_d, 1)

            def product(v, i):
                dve.wait_ge(up_mm, 6 * v + i + 1)
                dve.wait_ge(silu_d, 6 * v + i + 1)
                if i >= 2:
                    dve.wait_ge(h_lo_d, 6 * v + i - 1)
                for j in range(2):
                    ins = nc.vector.scalar_tensor_tensor(out=h32[:, i % 2, j * TOK:(j + 1) * TOK],
                                                         in0=b_up[:, j * TOK:(j + 1) * TOK],
                                                         scalar=us_t[:, 2 * i + j:2 * i + j + 1], in1=sil[:, j],
                                                         op0=ALU.mult, op1=ALU.mult)
                ins.then_inc(h_d, 1)

            def carry_and_state(s, c, m):
                dve.wait_ge(carry_mm, 2 * s + c + 1)
                nc.vector.tensor_tensor(o32[:, c], b_t[0][:, :], decay_q[:, :], ALU.mult).then_inc(carry_d, 1)
                dve.wait_ge(state_mm, 2 * s + c + 1)
                dve.wait_ge(state_dec, 2 * s + c + 1)
                if m == per_seq - 1 and c == T - 1:
                    nc.vector.memset(state[:, :, :], 0.0).then_inc(state_u, 1)
                else:
                    for j in range(HG):
                        r = slice(DH * j, DH * (j + 1))
                        ins = nc.vector.tensor_tensor(
                            state[r, :, r], b_t[1][r, :].rearrange("p (g n) -> p g n", g=KT)[:, :, r],
                            state_d[r, :, r], ALU.add)
                    ins.then_inc(state_u, 1)

            def out_sum(s, c):
                dve.wait_ge(att_mm, 2 * s + c + 1)
                dve.wait_ge(carry_d, 2 * s + c + 1)
                nc.vector.tensor_tensor(o32[:, c], b_att[:, :], o32[:, c], ALU.add).then_inc(o_d, 1)

            def v_sum(n, t):
                dve.wait_ge(v_mm, 2 * n + t + 1)
                nc.vector.tensor_tensor(v32[:, t], b_t[t][:, :], bv[:, :], ALU.add).then_inc(v_d, 1)

            def k_decay(n, c):
                dve.wait_ge(k_tr, 2 * n + c + 1)
                nc.vector.tensor_tensor(kd[:, c], b_t[c][:, :], decay_k[:, :], ALU.mult).then_inc(kd_d, 1)

            def y_moments(s, t):
                first = type(s) is int and s == 0
                dve.wait_ge(out_mm, 2 * s + t + 1)
                if first and t == 0:
                    dve.wait_ge(wout_in, 32)
                if not first:
                    dve.wait_ge(x1_d, 2 * s)
                nc.vector.scalar_tensor_tensor(out=y32[:, t], in0=(b_y, b_att)[t][:, :], scalar=col(13),
                                               in1=bo[:, :], op0=ALU.mult, op1=ALU.add).then_inc(y_d, 1)
                dve.wait_ge(y_d, 2 * s + t + 1)
                moments(LN_Y, 2 * s + t + 1, y32[:, t], t)

            def y_normalise(s, t):
                dve.wait_ge(rs_d[LN_Y], 2 * s + t + 1)
                normalise(LN_Y, y32[:, t], y32[:, t], t)

            def x1_moments(s, m, t):
                dve.wait_ge(x1_d, 2 * s + t + 1)
                moments(LN_X1, 2 * s + t + 1, x1[:, m % 2, t], t)

            def x1_normalise(s, m, t):
                dve.wait_ge(rs_d[LN_X1], 2 * s + t + 1)
                normalise(LN_X1, nrm[:, t], x1[:, m % 2, t], t)

            def y2_all(v, t):
                dve.wait_ge(down_mm, 2 * v + t + 1)
                dve.wait_ge(y2_free, v + 1)
                nc.vector.tensor_tensor(y2[:, t], (b_gate, b_up)[t][:, :], ds_t[:, :], ALU.mult
                                        ).then_inc(y2_d, 1)
                dve.wait_ge(y2_d, 2 * v + t + 1)
                moments(LN_Y2, 2 * v + t + 1, y2[:, t], t)
                dve.wait_ge(rs_d[LN_Y2], 2 * v + t + 1)
                normalise(LN_Y2, y2[:, t], y2[:, t], t)

            def slot(s, m, att, ffn, nxt):
                v = s - 1
                if ffn:
                    for j in range(2):
                        dve.wait_ge(x1_hi_d, 2 * v + j + 1)
                        nc.vector.tensor_tensor(x1_hl[:, 1, 2 * j:2 * j + 2].rearrange("p k t -> p (k t)"),
                                                (b_y, b_att)[j][:, :],
                                                x1_hl[:, 0, 2 * j:2 * j + 2].rearrange("p k t -> p (k t)"),
                                                ALU.subtract).then_inc(x1_lo_d, 1)
                if att:
                    masked(s, 0)
                if ffn:
                    product(v, 0)
                    product(v, 1)
                else:
                    for n in range(4):
                        quant(n)
                if att:
                    carry_and_state(s, 0, m)
                if nxt:
                    moments_x(s + 1, (m + 1) % 2)
                if ffn:
                    product(v, 2)
                if att:
                    out_sum(s, 0)
                    masked(s, 1)
                if nxt:
                    normalise_x(s + 1, (m + 1) % 2)
                if ffn:
                    product(v, 3)
                else:
                    for n in range(4, 8):
                        quant(n)
                if att:
                    carry_and_state(s, 1, m)
                if nxt:
                    x_lo(s + 1)
                if ffn:
                    product(v, 4)
                if att:
                    out_sum(s, 1)
                if ffn:
                    product(v, 5)
                else:
                    for n in range(8, 12):
                        quant(n)
                    quant_end(11)
                if att:
                    y_moments(s, 0)
                    y_normalise(s, 0)
                    x1_moments(s, m, 0)
                    x1_normalise(s, m, 0)
                if ffn:
                    y2_all(v, 0)
                if att:
                    y_moments(s, 1)
                    y_normalise(s, 1)
                if nxt:
                    v_sum(s + 1, 0)
                if att:
                    x1_moments(s, m, 1)
                if nxt:
                    v_sum(s + 1, 1)
                if att:
                    x1_normalise(s, m, 1)
                if nxt:
                    for c in range(T):
                        k_decay(s + 1, c)
                if ffn:
                    y2_all(v, 1)
                if not ffn:
                    scale_h()

            slots(dve.Fori, slot, start, lambda: None)


CONSTS = {}


def constants():
    first = 2.0 ** (-2.0 ** (-(np.log2(H) - 3)))
    slopes = np.array([first ** (i + 1) for i in range(H)], dtype=np.float32)
    lam = np.exp(-slopes).astype(np.float64)
    pos = np.arange(P, dtype=np.float64)
    diff = pos[None, :] - pos[:, None]
    mask = np.where(diff[:, None, :] >= 0, lam[None, :, None] ** np.maximum(diff, 0.0)[:, None, :], 0.0)
    per_channel = np.repeat(lam, DH)
    rows = (lam ** P).reshape(H // HG, HG).repeat(DH, axis=1).T
    return {
        "mask_c": mask * 2.0 ** -P_SHIFT,
        "decay_q_c": per_channel[None, :] ** (pos[:, None] + 1) * 2.0 ** -P_SHIFT,
        "decay_k_c": per_channel[None, :] ** (P - 1 - pos[:, None]),
        "lam_c": np.repeat(rows[:, :, None], P, axis=2),
        "eye_c": np.eye(P),
    }


def kernel(L0_attn_x, L0_attn_w_qkv, L0_attn_b_qkv, L0_attn_w_out, L0_attn_b_out, L0_ffn_gate_w, L0_ffn_up_w,
           L0_ffn_down_w, L0_ffn_gate_scale, L0_ffn_up_scale, L0_ffn_down_scale):
    import concourse.bacc as bacc
    from concourse.bass_utils import run_bass_kernel_spmd

    def rows(a):
        return np.broadcast_to(a[None, :], (P, a.shape[0]))

    def columns(a):
        return a.reshape(-1, P).T

    x = np.asarray(L0_attn_x)
    b_qkv = np.asarray(L0_attn_b_qkv)
    laid = {
        "x": x.reshape(-1, D),
        "w_qkv_t": np.asarray(L0_attn_w_qkv).T,
        "b_qk": columns(b_qkv[:2 * D]),
        "b_v": rows(b_qkv[2 * D:]),
        "w_out_t": np.asarray(L0_attn_w_out).T,
        "b_out": rows(np.asarray(L0_attn_b_out)),
        "gate_w": np.asarray(L0_ffn_gate_w),
        "up_w": np.asarray(L0_ffn_up_w),
        "down_w": np.asarray(L0_ffn_down_w),
        "gate_s": columns(np.asarray(L0_ffn_gate_scale)),
        "up_s": columns(np.asarray(L0_ffn_up_scale)),
        "down_s": rows(np.asarray(L0_ffn_down_scale)),
    }
    laid.update({name: a.astype(np.float32) for name, a in constants().items()})
    nc = bacc.Bacc("TRN2", target_bir_lowering=False, num_devices=1)
    arrays, args = {}, {}
    for name, a in laid.items():
        a = np.ascontiguousarray(a)
        arrays[f"in_{name}"] = a
        args[name] = nc.dram_tensor(f"in_{name}", a.shape, mybir.dt.from_np(a.dtype), kind="ExternalInput").ap()
    args["out"] = nc.dram_tensor("out_x", (x.shape[0] * x.shape[1], D), F32, kind="ExternalOutput").ap()
    sandwich(nc, **args)
    r = run_bass_kernel_spmd(nc, [arrays], core_ids=[0])
    return r.results[0]["out_x"].reshape(x.shape)
```

```python
from contextlib import ExitStack

import numpy as np

import concourse.bass as bass
from concourse import mybir

F32 = mybir.dt.float32
F16 = mybir.dt.float16
U32 = mybir.dt.uint32
ALU = mybir.AluOpType
ACT = mybir.ActivationFunctionType
AX = mybir.AxisListType
RMAX = bass.bass_isa.ReduceOp.max

P = 128
D = 512
KT = D // P
I = 1536
IT = I // P
H = 16
DH = D // H
HG = P // DH
TOK = 256
T = TOK // P
EPS = 1e-5
P_SHIFT = 20
EXPONENT = 0x7F800000
E4M3_TINY = 2.0 ** -6
E4M3_MAGIC = 1.5 * 2.0 ** 20
E4M3_FLOOR = E4M3_MAGIC * E4M3_TINY
E4M3_NAN = float(np.float32(3.4028235e38 / 464.0))


def sandwich(nc, x, w_qkv_t, b_qk, b_v, w_out_t, b_out, gate_w, up_w, down_w, gate_s, up_s, down_s,
             mask_c, decay_q_c, decay_k_c, lam_c, eye_c, out):
    units = x.shape[0] // TOK
    per_seq = 1024 // TOK
    x_u = x.rearrange("(n t p) d -> n p t d", t=T, p=P)
    out_u = out.rearrange("(n t p) d -> n t p d", t=T, p=P)

    with ExitStack() as ctx:
        def sb(name, shape, dt=F32):
            return ctx.enter_context(nc.sbuf_tensor(name, shape, dt))

        def sem(name):
            return ctx.enter_context(nc.semaphore(name))

        wqkv_hi = sb("wqkv_hi", [P, KT, 3 * D], F16)
        wqkv_lo = sb("wqkv_lo", [P, KT, 3 * D], F16)
        wout = sb("wout", [P, KT, D])
        gate_q = sb("gate_q", [P, KT, I], F16)
        up_q = sb("up_q", [P, KT, I], F16)
        down_q = sb("down_q", [P, IT, D], F16)
        mask = sb("mask", [P, H, P])
        decay_q = sb("decay_q", [P, D])
        decay_k = sb("decay_k", [P, D])
        lam = sb("lam", [P, KT, P])
        eye = sb("eye", [P, P])
        bqk = sb("bqk", [P, 2 * KT])
        bv = sb("bv", [P, D])
        bo = sb("bo", [P, D])
        ds_t = sb("ds_t", [P, D])
        gs_t = sb("gs_t", [P, IT])
        us_t = sb("us_t", [P, IT])
        small = sb("small", [P, 64])
        eps_t = sb("eps_t", [P, 2, T])

        x_t = sb("x_t", [P, 2, T, D])
        nrm = sb("nrm", [P, T, D])
        x_hl = sb("x_hl", [P, 2, KT, TOK], F16)
        qk = sb("qk", [P, 2 * KT, TOK])
        v32 = sb("v32", [P, T, D])
        v_hl = sb("v_hl", [P, 2, T, D], F16)
        kd = sb("kd", [P, T, D])
        p32 = sb("p32", [P, 2, D])
        o32 = sb("o32", [P, T, D])
        o_t = sb("o_t", [P, T, KT, P])
        y32 = sb("y32", [P, T, D])
        state = sb("state", [P, KT, P])
        state_d = sb("state_d", [P, KT, P])
        x1 = sb("x1", [P, 2, T, D])
        stats = sb("stats", [P, 4, T, 6])
        mv = sb("mv", [P, 4, T, 2])
        rstd = sb("rstd", [P, 4, 2, T])

        att_pool = sb("att_pool", [P, KT * 3 * D])
        stacks = att_pool[:, 0:2 * H * TOK // 2].bitcast(F16).rearrange(
            "p (s h t) -> p s h t", s=2, h=H)
        split = att_pool[:, 2 * H * TOK // 2:KT * 3 * D].bitcast(F16)
        qk_hl = split.rearrange("p (s k t) -> p s k t", s=2, k=2 * KT)
        pr_hl = split.rearrange("p (s h c) -> p s h c", s=2, h=H)
        w_stage = att_pool[:, :].rearrange("p (k n) -> p k n", k=KT)
        ffn_pool = sb("ffn_pool", [P, 7680])
        h_hl = ffn_pool[:, 0:3072].bitcast(F16).rearrange("p (s k t) -> p s k t", s=2, k=IT)
        sil = ffn_pool[:, 3072:3584].rearrange("p (j t) -> p j t", j=2)
        y2 = ffn_pool[:, 3584:4608].rearrange("p (t d) -> p t d", t=T)
        h32 = ffn_pool[:, 4608:5632].rearrange("p (i n) -> p i n", i=2)
        x1_hl = ffn_pool[:, 5632:6656].bitcast(F16).rearrange("p (s k t) -> p s k t", s=2, k=KT)
        f_stage = [ffn_pool[:, n * I:(n + 1) * I] for n in range(3)]
        f_magic = [ffn_pool[:, n * I:(n + 1) * I] for n in (3, 4)]

        bank = [ctx.enter_context(nc.psum_tensor(f"bank{n}", [P, D], F32)) for n in range(8)]
        b_gate, b_up, b_y, b_att = bank[0], bank[1], bank[2], bank[7]
        b_t = [bank[3], bank[4]]
        b_s = [bank[5], bank[6]]

        w_in = [sem(f"w_in{k}") for k in range(KT)]
        bias_in, tab_in, scl_in, wout_in = sem("bias_in"), sem("tab_in"), sem("scl_in"), sem("wout_in")
        f_in = [sem(f"f_in{n}") for n in range(3)]
        chain = sem("chain")
        w_max, w_max_all = sem("w_max"), sem("w_max_all")
        w_hi_d, w_lo_d = sem("w_hi_d"), sem("w_lo_d")
        f_exp_d, f_relu_d, f_magic_d, f_sum_d, f_q_d, f_max_d = (sem("f_exp_d"), sem("f_relu_d"), sem("f_magic_d"), sem("f_sum_d"),
                                                       sem("f_q_d"), sem("f_max_d"))
        eye_in, w_scale_d = sem("eye_in"), sem("w_scale_d")
        f_max, f_max_all = sem("f_max"), sem("f_max_all")
        bn_seen = sem("bn_seen")
        state_0, eps_d = sem("state_0"), sem("eps_d")
        x_in = [sem("x_in0"), sem("x_in1")]
        y2_free = sem("y2_free")
        q_stacked, k_stacked, stored = sem("q_stacked"), sem("k_stacked"), sem("stored")
        x_tr, qk_mm, v_mm, x1_tr, k_tr = sem("x_tr"), sem("qk_mm"), sem("v_mm"), sem("x1_tr"), sem("k_tr")
        score_mm, carry_mm, state_mm, att_mm = sem("score_mm"), sem("carry_mm"), sem("state_mm"), sem("att_mm")
        o_tr, out_mm, gate_mm, up_mm, down_mm = sem("o_tr"), sem("out_mm"), sem("gate_mm"), sem("up_mm"), sem("down_mm")
        x_hi_d, qk_d, qk_hi_d, v_hi_d, x1_hi_d = sem("x_hi_d"), sem("qk_d"), sem("qk_hi_d"), sem("v_hi_d"), sem("x1_hi_d")
        p_hi_d, o_t_d, silu_d, h_hi_d = sem("p_hi_d"), sem("o_t_d"), sem("silu_d"), sem("h_hi_d")
        x_lo_d, v_d, kd_d, x1_lo_d = sem("x_lo_d"), sem("v_d"), sem("kd_d"), sem("x1_lo_d")
        p_d, carry_d, state_u, o_d, h_d, y_d, y2_d = (sem("p_d"), sem("carry_d"), sem("state_u"), sem("o_d"),
                                                      sem("h_d"), sem("y_d"), sem("y2_d"))
        bn_d = [sem(f"bn_d{n}") for n in range(4)]
        mv_d = [sem(f"mv_d{n}") for n in range(4)]
        nrm_d = [sem(f"nrm_d{n}") for n in range(4)]
        qk_lo_d, v_lo_d, p_lo_d, h_lo_d = sem("qk_lo_d"), sem("v_lo_d"), sem("p_lo_d"), sem("h_lo_d")
        state_dec, x1_d, fin_d = sem("state_dec"), sem("x1_d"), sem("fin_d")
        ve_d = [sem(f"ve_d{n}") for n in range(4)]
        rs_d = [sem(f"rs_d{n}") for n in range(4)]

        N_BIAS, N_TAB, N_SCL = 2, 4, 3
        LN_X, LN_Y, LN_X1, LN_Y2 = range(4)
        last = units - 1

        def piece_in(n):
            w, k = (gate_w, up_w, down_w)[n // 4], n % 4
            if n < 8:
                return w[k * P:(k + 1) * P, :]
            return w[3 * k * P:3 * (k + 1) * P, :].rearrange("(c p) n -> p c n", p=P)

        def stage_for(n):
            return f_stage[n % 3] if n < 8 else f_stage[n % 3].rearrange("p (c n) -> p c n", n=D)

        def piece_out(n):
            if n < 8:
                return (gate_q, up_q)[n // 4][:, n % 4]
            return down_q[:, 3 * (n % 4):3 * (n % 4) + 3].rearrange("p c n -> p (c n)")

        def slots(fori, slot, start, end):
            start()
            slot(0, 0, att=True, ffn=False, nxt=True)
            slot(1, 1, att=True, ffn=True, nxt=True)
            with fori(0, (units - per_seq) // per_seq) as seq:
                for j in range(2, per_seq + 2):
                    slot(seq * per_seq + j, j % per_seq, att=True, ffn=True, nxt=True)
            for s in range(units - per_seq + 2, units + 1):
                slot(s, s % per_seq, att=s < units, ffn=True, nxt=s < last)
            end()

        def early(s):
            return type(s) is int and s < 2

        block = ctx.enter_context(nc.Block())

        @block.sync
        def _(sp):
            def start():
                sp.sem_inc(y2_free, 1)
                sp.dma_start(x_t[:, 0], x_u[0]).then_inc(x_in[0], 16)
                for k in range(KT):
                    sp.dma_start(w_stage[:, k], w_qkv_t[k * P:(k + 1) * P, :]).then_inc(w_in[k], 16)
                for dst, src in ((mask[:, :, :], mask_c), (decay_q[:, :], decay_q_c),
                                 (decay_k[:, :], decay_k_c), (lam[:, :, :], lam_c)):
                    sp.dma_start(dst, src).then_inc(tab_in, 16)
                sp.dma_start(wout[:, :, :], w_out_t.rearrange("(k p) n -> p k n", p=P)).then_inc(wout_in, 16)
                sp.dma_start(bo[:, :], b_out).then_inc(wout_in, 16)

            def stack(n):
                for which, done, parts in ((0, q_stacked, (0, 1, 0, 1)), (1, k_stacked, (0, 0, 1, 1))):
                    sp.wait_ge(qk_hi_d, 4 * n + 2 + 2 * which)
                    sp.wait_ge(qk_lo_d, 4 * n + 2 + 2 * which)
                    for j in range(HG):
                        for r in range(4):
                            sp.dma_start(stacks[DH * r:DH * (r + 1), which, j::HG, :],
                                         qk_hl[DH * j:DH * (j + 1), parts[r], KT * which:KT * (which + 1), :]
                                         ).then_inc(done, 16)

            def store(v, t):
                sp.wait_ge(fin_d, 2 * v + t + 1)
                sp.dma_start(out_u[v, t], y2[:, t]).then_inc(stored, 16)

            def store_last(v):
                store(v, T - 1)
                sp.wait_ge(stored, 16 * T * v + 16 * T)
                sp.sem_inc(y2_free, 1)

            def slot(s, m, att, ffn, nxt):
                if nxt:
                    if not (type(s) is int and s == 0):
                        sp.wait_ge(x1_d, 2 * s)
                    sp.dma_start(x_t[:, (m + 1) % 2], x_u[s + 1]).then_inc(x_in[(m + 1) % 2], 16)
                if not ffn:
                    stack(0)
                if not early(s):
                    store_last(s - 2)
                if nxt:
                    stack(s + 1)
                if ffn:
                    store(s - 1, 0)

            slots(sp.Fori, slot, start, lambda: store_last(last))

        @block.scalar
        def _(act):
            def start():
                act.dma_start(eye[:, :], eye_c).then_inc(eye_in, 16)
                act.dma_start(bqk[:, :], b_qk).then_inc(bias_in, 16)
                act.dma_start(bv[:, :], b_v).then_inc(bias_in, 16)
                for n in range(3):
                    act.dma_start(stage_for(n), piece_in(n)).then_inc(f_in[n], 16)
                act.dma_start(gs_t[:, :], gate_s).then_inc(scl_in, 16)
                act.dma_start(us_t[:, :], up_s).then_inc(scl_in, 16)
                act.dma_start(ds_t[:, :], down_s).then_inc(scl_in, 16)
                split_x(0)
                act.wait_ge(eps_d, 4)
                magic(0)
                act.wait_ge(w_scale_d, 1)
                for k in range(KT):
                    w_hi(wqkv_hi[:, k, 0:2 * D], w_stage[:, k, 0:2 * D])
                magic(1)
                w_hi(wqkv_hi[:, :, 2 * D:3 * D], w_stage[:, :, 2 * D:3 * D])
                act.wait_ge(w_lo_d, KT + 1)
                front(0, 0)
                front(0, 1)
                magic(2)
                front(0, 2)
                front(0, 3)
                magic(3)
                v_hi(0)
                magic(4)

            def w_hi(dst, src):
                nc.scalar.activation(dst, src, ACT.Copy, scale=small[:, 11:12]).then_inc(w_hi_d, 1)

            def magic(n):
                if 2 <= n < 11:
                    act.wait_ge(f_q_d, n - 1)
                    act.dma_start(stage_for(n + 1), piece_in(n + 1)).then_inc(f_in[(n + 1) % 3], 16)
                act.wait_ge(f_exp_d, n + 1)
                nc.scalar.activation(f_magic[n % 2], f_magic[n % 2], ACT.Relu, scale=E4M3_MAGIC,
                                     bias=small[:, 46:47]).then_inc(f_relu_d, 1)
                act.wait_ge(f_relu_d, n + 1)
                nc.scalar.activation(f_magic[n % 2], f_magic[n % 2], ACT.Identity, bias=small[:, 47:48]
                                     ).then_inc(f_magic_d, 1)

            def front(n, i):
                act.wait_ge(qk_mm, 4 * n + i + 1)
                for j in range(2):
                    o = 2 * i + j
                    ins = nc.scalar.activation(qk[:, o], b_t[i % 2][:, j * TOK:(j + 1) * TOK],
                                               ACT.Identity, bias=bqk[:, o:o + 1])
                ins.then_inc(qk_d, 1)
                act.wait_ge(qk_d, 4 * n + i + 1)
                nc.scalar.copy(qk_hl[:, 0, 2 * i:2 * i + 2].rearrange("p k t -> p (k t)"),
                               qk[:, 2 * i:2 * i + 2].rearrange("p k t -> p (k t)")).then_inc(qk_hi_d, 1)

            def v_hi(n):
                for t in range(T):
                    act.wait_ge(v_d, 2 * n + t + 1)
                    nc.scalar.copy(v_hl[:, 0, t], v32[:, t]).then_inc(v_hi_d, 1)

            def split_x(n):
                for j in range(2):
                    act.wait_ge(x_tr, 2 * n + j + 1)
                    nc.scalar.copy(x_hl[:, 0, 2 * j:2 * j + 2].rearrange("p k t -> p (k t)"),
                                   b_s[j][:, :]).then_inc(x_hi_d, 1)

            def probs_hi(s, c, half):
                if c and half == 0:
                    act.wait_ge(att_mm, 2 * s + 1)
                for g in range(2 * half, 2 * half + 2):
                    act.wait_ge(p_d, 8 * s + 4 * c + g + 1)
                    nc.scalar.copy(pr_hl[:, 0, 4 * g:4 * g + 4].rearrange("p h c -> p (h c)"),
                                   p32[:, g % 2]).then_inc(p_hi_d, 1)

            def silu(v, i):
                act.wait_ge(gate_mm, 6 * v + i + 1)
                if i:
                    act.wait_ge(h_d, 6 * v + i)
                for j in range(2):
                    ins = nc.scalar.activation(sil[:, j], b_gate[:, j * TOK:(j + 1) * TOK], ACT.Silu,
                                               scale=gs_t[:, 2 * i + j:2 * i + j + 1])
                ins.then_inc(silu_d, 1)

            def h_hi(v, i):
                act.wait_ge(h_d, 6 * v + i + 1)
                nc.scalar.copy(h_hl[:, 0, 2 * i:2 * i + 2].rearrange("p k t -> p (k t)"),
                               h32[:, i % 2]).then_inc(h_hi_d, 1)

            def out_t(s, c):
                act.wait_ge(o_tr, 2 * s + c + 1)
                nc.scalar.copy(o_t[:, c].rearrange("p k c -> p (k c)"), b_s[c][:, :]).then_inc(o_t_d, 1)

            def slot(s, m, att, ffn, nxt):
                v = s - 1
                if ffn:
                    for j in range(2):
                        act.wait_ge(x1_tr, 2 * v + j + 1)
                        nc.scalar.copy(x1_hl[:, 0, 2 * j:2 * j + 2].rearrange("p k t -> p (k t)"),
                                       (b_y, b_att)[j][:, :]).then_inc(x1_hi_d, 1)
                if att:
                    probs_hi(s, 0, 0)
                if ffn:
                    silu(v, 0)
                if att:
                    probs_hi(s, 0, 1)
                if ffn:
                    silu(v, 1)
                    h_hi(v, 0)
                    silu(v, 2)
                    h_hi(v, 1)
                if not ffn:
                    magic(5)
                if att:
                    probs_hi(s, 1, 0)
                if ffn:
                    silu(v, 3)
                    h_hi(v, 2)
                if att:
                    probs_hi(s, 1, 1)
                if ffn:
                    silu(v, 4)
                else:
                    magic(6)
                if nxt:
                    split_x(s + 1)
                if ffn:
                    h_hi(v, 3)
                    silu(v, 5)
                    h_hi(v, 4)
                    h_hi(v, 5)
                if att:
                    out_t(s, 0)
                    out_t(s, 1)
                if not ffn:
                    magic(7)
                if nxt:
                    for i in range(4):
                        front(s + 1, i)
                        if not ffn and i % 2:
                            magic(8 + i // 2)
                if not ffn:
                    magic(10)
                    magic(11)
                if nxt:
                    v_hi(s + 1)

            slots(act.Fori, slot, start, lambda: None)

        @block.tensor
        def _(pe):
            def transpose_x(n):
                pe.wait_ge(nrm_d[LN_X], 2 * n + 2)
                for j in range(2):
                    for kk in range(2):
                        for t in range(T):
                            ins = nc.tensor.transpose(b_s[j][:, kk * TOK + t * P:kk * TOK + (t + 1) * P],
                                                      nrm[:, t, (2 * j + kk) * P:(2 * j + kk + 1) * P], eye[:, :])
                    ins.then_inc(x_tr, 1)

            def start():
                pe.wait_ge(eye_in, 16)
                transpose_x(0)
                project_qk(0)
                project_v(0)
                transpose_k(0)
                pe.wait_ge(state_0, 1)

            def gate_up(v, i):
                if i == 0:
                    pe.wait_ge(x1_lo_d, 2 * v + 2)
                else:
                    pe.wait_ge(silu_d, 6 * v + i)
                for w, b, done in ((gate_q, b_gate, gate_mm), (up_q, b_up, up_mm)):
                    if done is up_mm and i:
                        pe.wait_ge(h_d, 6 * v + i)
                    for j in range(2):
                        o = 2 * i + j
                        for k in range(KT):
                            for part in range(2):
                                ins = nc.tensor.matmul(b[:, j * TOK:(j + 1) * TOK], w[:, k, o * P:(o + 1) * P],
                                                       x1_hl[:, part, k], start=(k == 0 and part == 0),
                                                       stop=(k == KT - 1 and part == 1))
                    ins.then_inc(done, 1)

            def down(v, t):
                pe.wait_ge(h_hi_d, 6 * v + 6)
                pe.wait_ge(h_lo_d, 6 * v + 6)
                for k in range(IT):
                    for part in range(2):
                        ins = nc.tensor.matmul((b_gate, b_up)[t][:, :], h_hl[:, part, k, t * P:(t + 1) * P],
                                               down_q[:, k], start=(k == 0 and part == 0),
                                               stop=(k == IT - 1 and part == 1))
                ins.then_inc(down_mm, 1)

            def scores(s, c, half):
                if c == 0 and half == 0:
                    pe.wait_ge(q_stacked, 256 * s + 256)
                    pe.wait_ge(k_stacked, 256 * s + 256)
                    if not (type(s) is int and s == 0):
                        pe.wait_ge(o_t_d, 2 * s)
                for g in range(2 * half, 2 * half + 2):
                    if c or half:
                        pe.wait_ge(p_d, 8 * s + 4 * c + g - 1)
                    for j in range(HG):
                        h = HG * g + j
                        ins = nc.tensor.matmul(b_s[g % 2][:, j * P:(j + 1) * P],
                                               stacks[:, 1, h, c * P:(c + 1) * P],
                                               stacks[:, 0, h, c * P:(c + 1) * P], start=True, stop=True)
                    ins.then_inc(score_mm, 1)

            def carry_and_state(s, c):
                if c == 0:
                    pe.wait_ge(kd_d, 2 * s + 2)
                else:
                    pe.wait_ge(carry_d, 2 * s + 1)
                if not (c == 0 and type(s) is int and s == 0):
                    pe.wait_ge(state_u, 2 * s + c)
                for g in range(KT):
                    ins = nc.tensor.matmul(b_t[0][:, g * P:(g + 1) * P], qk[:, g, c * P:(c + 1) * P],
                                           state[:, g], start=True, stop=True)
                ins.then_inc(carry_mm, 1)
                for g in range(KT):
                    ins = nc.tensor.matmul(b_t[1][:, g * P:(g + 1) * P], kd[:, c, g * P:(g + 1) * P],
                                           v32[:, c, g * P:(g + 1) * P], start=True, stop=True)
                ins.then_inc(state_mm, 1)

            def attend(s, c):
                pe.wait_ge(p_hi_d, 8 * s + 4 * c + 4)
                pe.wait_ge(p_lo_d, 8 * s + 4 * c + 4)
                pe.wait_ge(v_hi_d, 2 * s + c + 1)
                pe.wait_ge(v_lo_d, 2 * s + c + 1)
                if c:
                    pe.wait_ge(o_d, 2 * s + 1)
                for h in range(H):
                    for n, (a, b) in enumerate(((0, 0), (0, 1), (1, 0))):
                        ins = nc.tensor.matmul(b_att[:, h * DH:(h + 1) * DH], pr_hl[:, a, h],
                                               v_hl[:, b, c, h * DH:(h + 1) * DH], start=(n == 0), stop=(n == 2))
                ins.then_inc(att_mm, 1)

            def transpose_o(s, c, nxt):
                pe.wait_ge(o_d, 2 * s + c + 1)
                if nxt:
                    pe.wait_ge(x_lo_d, 2 * s + 4)
                elif c == 0:
                    pe.wait_ge(p_d, 8 * s + 8)
                for k in range(KT):
                    ins = nc.tensor.transpose(b_s[c][:, k * P:(k + 1) * P], o32[:, c, k * P:(k + 1) * P], eye[:, :])
                ins.then_inc(o_tr, 1)

            def project(s, c):
                pe.wait_ge(o_t_d, 2 * s + c + 1)
                for k in range(KT):
                    ins = nc.tensor.matmul((b_y, b_att)[c][:, :], o_t[:, c, k], wout[:, k], start=(k == 0),
                                           stop=(k == KT - 1))
                ins.then_inc(out_mm, 1)

            def project_qk(n):
                first = type(n) is int and n == 0
                pe.wait_ge(x_lo_d, 2 * n + 2)
                for i in range(4):
                    if i >= 2:
                        pe.wait_ge(qk_d, 4 * n + i - 1)
                    elif not first:
                        pe.wait_ge((carry_d, state_u)[i], 2 * n)
                    for j in range(2):
                        o = 2 * i + j
                        for k in range(KT):
                            if first and i == 0 and j == 0:
                                pe.wait_ge(w_hi_d, k + 1)
                                pe.wait_ge(w_lo_d, k + 1)
                            for q, (a, b) in enumerate(((0, 0), (0, 1), (1, 0))):
                                ins = nc.tensor.matmul(b_t[i % 2][:, j * TOK:(j + 1) * TOK],
                                                       (wqkv_hi, wqkv_lo)[a][:, k, o * P:(o + 1) * P],
                                                       x_hl[:, b, k], start=(k == 0 and q == 0),
                                                       stop=(k == KT - 1 and q == 2))
                    ins.then_inc(qk_mm, 1)

            def project_v(n):
                if type(n) is int and n == 0:
                    pe.wait_ge(w_hi_d, KT + 1)
                    pe.wait_ge(w_lo_d, KT + 1)
                for t in range(T):
                    pe.wait_ge(qk_d, 4 * n + 3 + t)
                    for k in range(KT):
                        for q, (a, b) in enumerate(((0, 0), (0, 1), (1, 0))):
                            ins = nc.tensor.matmul(b_t[t][:, :], x_hl[:, b, k, t * P:(t + 1) * P],
                                                   (wqkv_hi, wqkv_lo)[a][:, k, 2 * D:3 * D],
                                                   start=(k == 0 and q == 0), stop=(k == KT - 1 and q == 2))
                    ins.then_inc(v_mm, 1)

            def transpose_k(n):
                for c in range(T):
                    pe.wait_ge(v_d, 2 * n + c + 1)
                    for g in range(KT):
                        ins = nc.tensor.transpose(b_t[c][:, g * P:(g + 1) * P],
                                                  qk[:, KT + g, c * P:(c + 1) * P], eye[:, :])
                    ins.then_inc(k_tr, 1)

            def slot(s, m, att, ffn, nxt):
                v = s - 1
                if ffn:
                    pe.wait_ge(nrm_d[LN_X1], 2 * v + 2)
                    for j in range(2):
                        for kk in range(2):
                            for t in range(T):
                                ins = nc.tensor.transpose((b_y, b_att)[j][:, kk * TOK + t * P:kk * TOK + (t + 1) * P],
                                                          nrm[:, t, (2 * j + kk) * P:(2 * j + kk + 1) * P], eye[:, :])
                        ins.then_inc(x1_tr, 1)
                if att:
                    scores(s, 0, 0)
                    carry_and_state(s, 0)
                if ffn:
                    gate_up(v, 0)
                if att:
                    scores(s, 0, 1)
                if ffn:
                    gate_up(v, 1)
                    gate_up(v, 2)
                if att:
                    attend(s, 0)
                    scores(s, 1, 0)
                if ffn:
                    gate_up(v, 3)
                if att:
                    scores(s, 1, 1)
                    carry_and_state(s, 1)
                if ffn:
                    gate_up(v, 4)
                if nxt:
                    pe.wait_ge(p_d, 8 * s + 8)
                    transpose_x(s + 1)
                if att:
                    attend(s, 1)
                if ffn:
                    gate_up(v, 5)
                if att:
                    transpose_o(s, 0, nxt)
                    transpose_o(s, 1, nxt)
                if nxt:
                    project_qk(s + 1)
                if att:
                    if type(s) is int and s == 0:
                        pe.wait_ge(wout_in, 32)
                    project(s, 0)
                if ffn:
                    down(v, 0)
                if att:
                    project(s, 1)
                if nxt:
                    project_v(s + 1)
                if ffn:
                    down(v, 1)
                if nxt:
                    transpose_k(s + 1)

            slots(pe.Fori, slot, start, lambda: None)

        @block.gpsimd
        def _(pool):
            def inverse_std(ln, val, cols):
                nc.gpsimd.tensor_tensor(rstd[:, ln, 0, cols], mv[:, ln, cols, 1], eps_t[:, 0, cols],
                                        ALU.add).then_inc(ve_d[ln], 1)
                pool.wait_ge(ve_d[ln], val)
                nc.gpsimd.tensor_tensor(rstd[:, ln, 1, cols], rstd[:, ln, 0, cols], eps_t[:, 1, cols],
                                        ALU.pow).then_inc(rs_d[ln], 1)

            def inverse_std_x(n):
                pool.wait_ge(mv_d[LN_X], 2 * n + 2)
                inverse_std(LN_X, n + 1, slice(0, T))

            def start():
                nc.gpsimd.memset(eps_t[:, 0, :], EPS).then_inc(eps_d, 1)
                nc.gpsimd.memset(eps_t[:, 1, :], -0.5).then_inc(eps_d, 1)
                nc.gpsimd.memset(small[:, 46:47], -E4M3_FLOOR).then_inc(eps_d, 1)
                nc.gpsimd.memset(small[:, 47:48], E4M3_FLOOR).then_inc(eps_d, 1)
                nc.gpsimd.memset(state[:, :, :], 0.0).then_inc(state_0, 1)
                pool.wait_ge(eps_d, 4)
                inverse_std_x(0)
                pool.wait_ge(w_max, 1)
                nc.gpsimd.partition_all_reduce(small[:, 6:7], small[:, 5:6], P, RMAX).then_inc(w_max_all, 1)
                pool.wait_ge(state_0, 1)
                quant_sum(0)
                quant_sum(1)
                qk_lo(0, 0)
                qk_lo(0, 1)
                quant_sum(2)
                qk_lo(0, 2)
                qk_lo(0, 3)
                quant_sum(3)
                v_lo(0)

            def quant_sum(n):
                pool.wait_ge(f_magic_d, n + 1)
                nc.gpsimd.tensor_tensor(f_stage[n % 3], f_stage[n % 3], f_magic[n % 2], ALU.add
                                        ).then_inc(f_sum_d, 1)

            def h_lo(v, i):
                pool.wait_ge(h_hi_d, 6 * v + i + 1)
                nc.gpsimd.tensor_tensor(h_hl[:, 1, 2 * i:2 * i + 2].rearrange("p k t -> p (k t)"), h32[:, i % 2],
                                        h_hl[:, 0, 2 * i:2 * i + 2].rearrange("p k t -> p (k t)"),
                                        ALU.subtract).then_inc(h_lo_d, 1)

            def state_decay(s, c):
                if not (c == 0 and type(s) is int and s == 0):
                    pool.wait_ge(state_u, 2 * s + c)
                nc.gpsimd.tensor_tensor(state_d[:, :, :], state[:, :, :], lam[:, :, :], ALU.mult
                                        ).then_inc(state_dec, 1)

            def probs_lo(s, c, half):
                for g in range(2 * half, 2 * half + 2):
                    pool.wait_ge(p_hi_d, 8 * s + 4 * c + g + 1)
                    nc.gpsimd.tensor_tensor(pr_hl[:, 1, 4 * g:4 * g + 4].rearrange("p h c -> p (h c)"), p32[:, g % 2],
                                            pr_hl[:, 0, 4 * g:4 * g + 4].rearrange("p h c -> p (h c)"),
                                            ALU.subtract).then_inc(p_lo_d, 1)

            def qk_lo(n, i):
                pool.wait_ge(qk_hi_d, 4 * n + i + 1)
                nc.gpsimd.tensor_tensor(qk_hl[:, 1, 2 * i:2 * i + 2].rearrange("p k t -> p (k t)"),
                                        qk[:, 2 * i:2 * i + 2].rearrange("p k t -> p (k t)"),
                                        qk_hl[:, 0, 2 * i:2 * i + 2].rearrange("p k t -> p (k t)"),
                                        ALU.subtract).then_inc(qk_lo_d, 1)

            def v_lo(n):
                for t in range(T):
                    pool.wait_ge(v_hi_d, 2 * n + t + 1)
                    nc.gpsimd.tensor_tensor(v_hl[:, 1, t], v32[:, t], v_hl[:, 0, t], ALU.subtract
                                            ).then_inc(v_lo_d, 1)

            def y2_inverse_std(v, t):
                pool.wait_ge(mv_d[LN_Y2], 2 * v + t + 1)
                inverse_std(LN_Y2, 2 * v + t + 1, slice(t, t + 1))

            def final(v, par, t):
                pool.wait_ge(nrm_d[LN_Y2], 2 * v + t + 1)
                nc.gpsimd.tensor_tensor(y2[:, t], x1[:, par, t], y2[:, t], ALU.add).then_inc(fin_d, 1)

            def slot(s, m, att, ffn, nxt):
                v = s - 1
                if att:
                    if not ffn:
                        quant_sum(4)
                        pool.wait_ge(tab_in, 16 * N_TAB)
                    state_decay(s, 0)
                    probs_lo(s, 0, 0)
                if not early(s):
                    y2_inverse_std(s - 2, 1)
                if att:
                    probs_lo(s, 0, 1)
                if not early(s):
                    final(s - 2, m % 2, 1)
                if ffn:
                    for i in range(2):
                        h_lo(v, i)
                else:
                    quant_sum(5)
                if nxt:
                    inverse_std_x(s + 1)
                if att:
                    state_decay(s, 1)
                if ffn:
                    h_lo(v, 2)
                if att:
                    probs_lo(s, 1, 0)
                    probs_lo(s, 1, 1)
                if ffn:
                    for i in range(3, 6):
                        h_lo(v, i)
                else:
                    quant_sum(6)
                    quant_sum(7)
                if nxt:
                    for i in range(4):
                        qk_lo(s + 1, i)
                        if not ffn and i == 1:
                            quant_sum(8)
                for t in range(T):
                    if att:
                        pool.wait_ge(mv_d[LN_Y], 2 * s + t + 1)
                        inverse_std(LN_Y, 2 * s + t + 1, slice(t, t + 1))
                        pool.wait_ge(nrm_d[LN_Y], 2 * s + t + 1)
                        nc.gpsimd.tensor_tensor(x1[:, m % 2, t], x_t[:, m % 2, t], y32[:, t], ALU.add
                                                ).then_inc(x1_d, 1)
                        if not ffn and t == 0:
                            quant_sum(9)
                        pool.wait_ge(mv_d[LN_X1], 2 * s + t + 1)
                        inverse_std(LN_X1, 2 * s + t + 1, slice(t, t + 1))
                        if not ffn:
                            quant_sum(10 + t)
                    if ffn and t == 0:
                        y2_inverse_std(v, 0)
                        final(v, (m + 1) % 2, 0)
                if nxt:
                    v_lo(s + 1)
                if not ffn:
                    pool.wait_ge(f_max, 1)
                    nc.gpsimd.partition_all_reduce(small[:, 36:41], small[:, 19:24], P, RMAX).then_inc(f_max_all, 1)

            def end():
                y2_inverse_std(last, 1)
                final(last, last % 2, 1)

            slots(pool.Fori, slot, start, end)

        @block.vector
        def _(dve):
            links = [0]

            def link(ins):
                links[0] += 1
                ins.then_inc(chain, 1)
                dve.wait_ge(chain, links[0])

            def col(a, n=1):
                return small[:, a:a + n]

            def power_of_two(dst, src, low, high):
                link(nc.vector.tensor_scalar(dst.bitcast(U32), src.bitcast(U32), EXPONENT, None, ALU.bitwise_and))
                link(nc.vector.tensor_scalar(dst, dst, low, high, ALU.max, ALU.min))

            def prepare_qkv():
                for k in range(KT):
                    dve.wait_ge(w_in[k], 16)
                    nc.vector.tensor_reduce(col(k), w_stage[:, k], AX.X, ALU.max, apply_absolute_value=True)
                dve.wait_ge(bias_in, 16 * N_BIAS)
                nc.vector.tensor_reduce(col(7), bqk[:, :], AX.X, ALU.max, apply_absolute_value=True)
                link(nc.vector.tensor_reduce(col(8), bv[:, :], AX.X, ALU.max, apply_absolute_value=True))
                link(nc.vector.tensor_tensor(col(7), col(7), col(8), ALU.max))
                link(nc.vector.tensor_scalar(col(4), col(7), 1.0 / 256.0, None, ALU.mult))
                nc.vector.tensor_reduce(col(5), col(0, 5), AX.X, ALU.max).then_inc(w_max, 1)
                exponents(0)
                dve.wait_ge(w_max_all, 1)
                power_of_two(col(9), col(6), 2.0 ** -30, 2.0 ** 35)
                link(nc.vector.tensor_scalar(col(10), col(9), 2.0 ** -5, None, ALU.mult))
                nc.vector.reciprocal(col(11), col(10)).then_inc(w_scale_d, 1)
                dve.wait_ge(w_scale_d, 1)
                nc.vector.tensor_scalar(bqk[:, :], bqk[:, :], col(11), None, ALU.mult)
                link(nc.vector.tensor_scalar(bv[:, :], bv[:, :], col(11), None, ALU.mult))
                x_lo(0)
                w_lo(0, wqkv_lo[:, 0, 0:2 * D], wqkv_hi[:, 0, 0:2 * D], w_stage[:, 0, 0:2 * D])
                w_lo(1, wqkv_lo[:, 1, 0:2 * D], wqkv_hi[:, 1, 0:2 * D], w_stage[:, 1, 0:2 * D])
                exponents(1)
                for k in range(2, KT):
                    w_lo(k, wqkv_lo[:, k, 0:2 * D], wqkv_hi[:, k, 0:2 * D], w_stage[:, k, 0:2 * D])
                w_lo(KT, wqkv_lo[:, :, 2 * D:3 * D], wqkv_hi[:, :, 2 * D:3 * D], w_stage[:, :, 2 * D:3 * D])
                link(nc.vector.tensor_tensor(col(12), col(10), col(10), ALU.mult))
                link(nc.vector.scalar_tensor_tensor(out=col(13), in0=col(12), scalar=2.0 ** P_SHIFT, in1=col(10),
                                                    op0=ALU.mult, op1=ALU.mult))

            def w_lo(n, lo, hi, src):
                dve.wait_ge(w_hi_d, n + 1)
                nc.vector.scalar_tensor_tensor(out=lo, in0=src, scalar=col(11), in1=hi, op0=ALU.mult,
                                               op1=ALU.subtract).then_inc(w_lo_d, 1)

            def exponents(n):
                dve.wait_ge(f_in[n % 3], 16 * (n // 3 + 1))
                if n >= 2:
                    dve.wait_ge(f_q_d, n - 1)
                nc.vector.tensor_scalar(f_magic[n % 2].bitcast(U32), f_stage[n % 3].bitcast(U32), EXPONENT, None,
                                        ALU.bitwise_and).then_inc(f_exp_d, 1)

            def rounded(n):
                dve.wait_ge(f_sum_d, n + 1)
                nc.vector.tensor_tensor(piece_out(n), f_stage[n % 3], f_magic[n % 2], ALU.subtract
                                        ).then_inc(f_q_d, 1)

            def maximum(n):
                dve.wait_ge(f_q_d, n + 1)
                nc.vector.tensor_reduce(col(24 + n), piece_out(n), AX.X, ALU.max, apply_absolute_value=True
                                        ).then_inc(f_max_d, 1)

            def quant(n):
                exponents(n)
                rounded(n - 1)
                if n >= 2:
                    maximum(n - 2)

            def scale_h():
                dve.wait_ge(scl_in, 16 * N_SCL)
                dve.wait_ge(f_max_d, 12)
                for w in range(3):
                    nc.vector.tensor_reduce(col(19 + w), col(24 + 4 * w, 4), AX.X, ALU.max)
                nc.vector.tensor_reduce(col(22), gs_t[:, :], AX.X, ALU.max, apply_absolute_value=True)
                nc.vector.tensor_reduce(col(23), us_t[:, :], AX.X, ALU.max, apply_absolute_value=True
                                        ).then_inc(f_max, 1)
                dve.wait_ge(f_max_all, 1)
                link(nc.vector.tensor_tensor(col(50), col(36), col(37), ALU.mult))
                link(nc.vector.tensor_tensor(col(51), col(39), col(40), ALU.mult))
                link(nc.vector.scalar_tensor_tensor(out=col(52), in0=col(50), scalar=float(D * D), in1=col(51),
                                                    op0=ALU.mult, op1=ALU.mult))
                power_of_two(col(53), col(52), 2.0 ** -60, 2.0 ** 100)
                link(nc.vector.tensor_scalar(col(54), col(53), 2.0 ** -14, None, ALU.mult))
                link(nc.vector.reciprocal(col(55), col(54)))
                link(nc.vector.tensor_reduce(col(56), col(36, 3), AX.X, ALU.max))
                link(nc.vector.tensor_scalar(col(57), col(56), E4M3_NAN, 0.0, ALU.mult, ALU.mult))
                nc.vector.tensor_scalar(us_t[:, :], us_t[:, :], col(55), None, ALU.mult)
                link(nc.vector.tensor_scalar(ds_t[:, :], ds_t[:, :], col(54), col(57), ALU.mult, ALU.add))

            def moments(ln, val, src, t):
                nc.vector.bn_stats(stats[:, ln, t], src).then_inc(bn_d[ln], 1)
                dve.wait_ge(bn_d[ln], val)
                dve.sem_inc(bn_seen, 1)
                nc.vector.bn_aggr(mv[:, ln, t], stats[:, ln, t]).then_inc(mv_d[ln], 1)

            def normalise(ln, dst, src, t):
                nc.vector.tensor_scalar(dst, src, mv[:, ln, t, 0:1], rstd[:, ln, 1, t:t + 1], ALU.subtract,
                                        ALU.mult).then_inc(nrm_d[ln], 1)

            def moments_x(n, par):
                dve.wait_ge(x_in[par], 8 * (n - par) + 16)
                for t in range(T):
                    moments(LN_X, 2 * n + t + 1, x_t[:, par, t], t)

            def normalise_x(n, par):
                dve.wait_ge(rs_d[LN_X], n + 1)
                for t in range(T):
                    normalise(LN_X, nrm[:, t], x_t[:, par, t], t)

            def x_lo(n):
                for j in range(2):
                    dve.wait_ge(x_hi_d, 2 * n + j + 1)
                    nc.vector.tensor_tensor(x_hl[:, 1, 2 * j:2 * j + 2].rearrange("p k t -> p (k t)"), b_s[j][:, :],
                                            x_hl[:, 0, 2 * j:2 * j + 2].rearrange("p k t -> p (k t)"),
                                            ALU.subtract).then_inc(x_lo_d, 1)

            def start():
                moments_x(0, 0)
                normalise_x(0, 0)
                prepare_qkv()
                rounded(0)
                exponents(2)
                rounded(1)
                maximum(0)
                quant(3)
                for t in range(T):
                    v_sum(0, t)
                quant(4)
                dve.wait_ge(tab_in, 16 * N_TAB)
                for c in range(T):
                    k_decay(0, c)

            def masked(s, c, half):
                for g in range(2 * half, 2 * half + 2):
                    dve.wait_ge(score_mm, 8 * s + 4 * c + g + 1)
                    if not (type(s) is int and s == 0 and c == 0 and g < 2):
                        dve.wait_ge(p_lo_d, 8 * s + 4 * c + g - 1)
                    nc.vector.tensor_tensor(p32[:, g % 2], b_s[g % 2][:, :],
                                            mask[:, HG * g:HG * (g + 1)].rearrange("p h c -> p (h c)"),
                                            ALU.mult).then_inc(p_d, 1)

            def product(v, i):
                dve.wait_ge(up_mm, 6 * v + i + 1)
                dve.wait_ge(silu_d, 6 * v + i + 1)
                if i >= 2:
                    dve.wait_ge(h_lo_d, 6 * v + i - 1)
                for j in range(2):
                    ins = nc.vector.scalar_tensor_tensor(out=h32[:, i % 2, j * TOK:(j + 1) * TOK],
                                                         in0=b_up[:, j * TOK:(j + 1) * TOK],
                                                         scalar=us_t[:, 2 * i + j:2 * i + j + 1], in1=sil[:, j],
                                                         op0=ALU.mult, op1=ALU.mult)
                ins.then_inc(h_d, 1)

            def carry_and_state(s, c, m):
                dve.wait_ge(carry_mm, 2 * s + c + 1)
                nc.vector.tensor_tensor(o32[:, c], b_t[0][:, :], decay_q[:, :], ALU.mult).then_inc(carry_d, 1)
                dve.wait_ge(state_mm, 2 * s + c + 1)
                dve.wait_ge(state_dec, 2 * s + c + 1)
                if m == per_seq - 1 and c == T - 1:
                    nc.vector.memset(state[:, :, :], 0.0).then_inc(state_u, 1)
                else:
                    for j in range(HG):
                        r = slice(DH * j, DH * (j + 1))
                        ins = nc.vector.tensor_tensor(
                            state[r, :, r], b_t[1][r, :].rearrange("p (g n) -> p g n", g=KT)[:, :, r],
                            state_d[r, :, r], ALU.add)
                    ins.then_inc(state_u, 1)

            def out_sum(s, c):
                dve.wait_ge(att_mm, 2 * s + c + 1)
                dve.wait_ge(carry_d, 2 * s + c + 1)
                nc.vector.tensor_tensor(o32[:, c], b_att[:, :], o32[:, c], ALU.add).then_inc(o_d, 1)

            def v_sum(n, t):
                dve.wait_ge(v_mm, 2 * n + t + 1)
                nc.vector.tensor_tensor(v32[:, t], b_t[t][:, :], bv[:, :], ALU.add).then_inc(v_d, 1)

            def k_decay(n, c):
                dve.wait_ge(k_tr, 2 * n + c + 1)
                nc.vector.tensor_tensor(kd[:, c], b_t[c][:, :], decay_k[:, :], ALU.mult).then_inc(kd_d, 1)

            def y_moments(s, t):
                first = type(s) is int and s == 0
                dve.wait_ge(out_mm, 2 * s + t + 1)
                if first and t == 0:
                    dve.wait_ge(wout_in, 32)
                if not first:
                    dve.wait_ge(x1_d, 2 * s)
                nc.vector.scalar_tensor_tensor(out=y32[:, t], in0=(b_y, b_att)[t][:, :], scalar=col(13),
                                               in1=bo[:, :], op0=ALU.mult, op1=ALU.add).then_inc(y_d, 1)
                dve.wait_ge(y_d, 2 * s + t + 1)
                moments(LN_Y, 2 * s + t + 1, y32[:, t], t)

            def y_normalise(s, t):
                dve.wait_ge(rs_d[LN_Y], 2 * s + t + 1)
                normalise(LN_Y, y32[:, t], y32[:, t], t)

            def x1_moments(s, m, t):
                dve.wait_ge(x1_d, 2 * s + t + 1)
                moments(LN_X1, 2 * s + t + 1, x1[:, m % 2, t], t)

            def x1_normalise(s, m, t):
                dve.wait_ge(rs_d[LN_X1], 2 * s + t + 1)
                normalise(LN_X1, nrm[:, t], x1[:, m % 2, t], t)

            def y2_scale(v, t):
                dve.wait_ge(down_mm, 2 * v + t + 1)
                dve.wait_ge(y2_free, v + 1)
                nc.vector.tensor_tensor(y2[:, t], (b_gate, b_up)[t][:, :], ds_t[:, :], ALU.mult
                                        ).then_inc(y2_d, 1)

            def y2_moments(v, t):
                dve.wait_ge(y2_d, 2 * v + t + 1)
                moments(LN_Y2, 2 * v + t + 1, y2[:, t], t)

            def y2_normalise(v, t):
                dve.wait_ge(rs_d[LN_Y2], 2 * v + t + 1)
                normalise(LN_Y2, y2[:, t], y2[:, t], t)

            def slot(s, m, att, ffn, nxt):
                v = s - 1
                if ffn:
                    for j in range(2):
                        dve.wait_ge(x1_hi_d, 2 * v + j + 1)
                        nc.vector.tensor_tensor(x1_hl[:, 1, 2 * j:2 * j + 2].rearrange("p k t -> p (k t)"),
                                                (b_y, b_att)[j][:, :],
                                                x1_hl[:, 0, 2 * j:2 * j + 2].rearrange("p k t -> p (k t)"),
                                                ALU.subtract).then_inc(x1_lo_d, 1)
                if att:
                    masked(s, 0, 0)
                    carry_and_state(s, 0, m)
                if not early(s):
                    y2_moments(s - 2, 1)
                if ffn:
                    product(v, 0)
                if att:
                    masked(s, 0, 1)
                if not early(s):
                    y2_normalise(s - 2, 1)
                if ffn:
                    product(v, 1)
                else:
                    quant(5)
                if nxt:
                    moments_x(s + 1, (m + 1) % 2)
                if ffn:
                    product(v, 2)
                if att:
                    out_sum(s, 0)
                    masked(s, 1, 0)
                if nxt:
                    normalise_x(s + 1, (m + 1) % 2)
                if ffn:
                    product(v, 3)
                if att:
                    masked(s, 1, 1)
                if not ffn:
                    quant(6)
                if att:
                    carry_and_state(s, 1, m)
                if ffn:
                    product(v, 4)
                if nxt:
                    x_lo(s + 1)
                if att:
                    out_sum(s, 1)
                if ffn:
                    product(v, 5)
                else:
                    for n in (7, 8, 9):
                        quant(n)
                if att:
                    y_moments(s, 0)
                    y_normalise(s, 0)
                    if not ffn:
                        quant(10)
                    x1_moments(s, m, 0)
                    x1_normalise(s, m, 0)
                if ffn:
                    y2_scale(v, 0)
                    y2_moments(v, 0)
                    y2_normalise(v, 0)
                if att:
                    y_moments(s, 1)
                    y_normalise(s, 1)
                if nxt:
                    v_sum(s + 1, 0)
                if not ffn:
                    quant(11)
                if att:
                    x1_moments(s, m, 1)
                if nxt:
                    v_sum(s + 1, 1)
                if att:
                    x1_normalise(s, m, 1)
                if ffn:
                    y2_scale(v, 1)
                if nxt:
                    for c in range(T):
                        k_decay(s + 1, c)
                if not ffn:
                    rounded(11)
                    maximum(10)
                    maximum(11)
                    scale_h()

            def end():
                y2_moments(last, 1)
                y2_normalise(last, 1)

            slots(dve.Fori, slot, start, end)


CONSTS = {}


def constants():
    first = 2.0 ** (-2.0 ** (-(np.log2(H) - 3)))
    slopes = np.array([first ** (i + 1) for i in range(H)], dtype=np.float32)
    lam = np.exp(-slopes).astype(np.float64)
    pos = np.arange(P, dtype=np.float64)
    diff = pos[None, :] - pos[:, None]
    mask = np.where(diff[:, None, :] >= 0, lam[None, :, None] ** np.maximum(diff, 0.0)[:, None, :], 0.0)
    per_channel = np.repeat(lam, DH)
    rows = (lam ** P).reshape(H // HG, HG).repeat(DH, axis=1).T
    return {
        "mask_c": mask * 2.0 ** -P_SHIFT,
        "decay_q_c": per_channel[None, :] ** (pos[:, None] + 1) * 2.0 ** -P_SHIFT,
        "decay_k_c": per_channel[None, :] ** (P - 1 - pos[:, None]),
        "lam_c": np.repeat(rows[:, :, None], P, axis=2),
        "eye_c": np.eye(P),
    }


def kernel(L0_attn_x, L0_attn_w_qkv, L0_attn_b_qkv, L0_attn_w_out, L0_attn_b_out, L0_ffn_gate_w, L0_ffn_up_w,
           L0_ffn_down_w, L0_ffn_gate_scale, L0_ffn_up_scale, L0_ffn_down_scale):
    import concourse.bacc as bacc
    from concourse.bass_utils import run_bass_kernel_spmd

    def rows(a):
        return np.broadcast_to(a[None, :], (P, a.shape[0]))

    def columns(a):
        return a.reshape(-1, P).T

    x = np.asarray(L0_attn_x)
    b_qkv = np.asarray(L0_attn_b_qkv)
    laid = {
        "x": x.reshape(-1, D),
        "w_qkv_t": np.asarray(L0_attn_w_qkv).T,
        "b_qk": columns(b_qkv[:2 * D]),
        "b_v": rows(b_qkv[2 * D:]),
        "w_out_t": np.asarray(L0_attn_w_out).T,
        "b_out": rows(np.asarray(L0_attn_b_out)),
        "gate_w": np.asarray(L0_ffn_gate_w),
        "up_w": np.asarray(L0_ffn_up_w),
        "down_w": np.asarray(L0_ffn_down_w),
        "gate_s": columns(np.asarray(L0_ffn_gate_scale)),
        "up_s": columns(np.asarray(L0_ffn_up_scale)),
        "down_s": rows(np.asarray(L0_ffn_down_scale)),
    }
    laid.update({name: a.astype(np.float32) for name, a in constants().items()})
    nc = bacc.Bacc("TRN2", target_bir_lowering=False, num_devices=1)
    arrays, args = {}, {}
    for name, a in laid.items():
        a = np.ascontiguousarray(a)
        arrays[f"in_{name}"] = a
        args[name] = nc.dram_tensor(f"in_{name}", a.shape, mybir.dt.from_np(a.dtype), kind="ExternalInput").ap()
    args["out"] = nc.dram_tensor("out_x", (x.shape[0] * x.shape[1], D), F32, kind="ExternalOutput").ap()
    sandwich(nc, **args)
    r = run_bass_kernel_spmd(nc, [arrays], core_ids=[0])
    return r.results[0]["out_x"].reshape(x.shape)
```

```python
from contextlib import ExitStack

import numpy as np

import concourse.bass as bass
from concourse import mybir

F32 = mybir.dt.float32
F16 = mybir.dt.float16
U32 = mybir.dt.uint32
ALU = mybir.AluOpType
ACT = mybir.ActivationFunctionType
AX = mybir.AxisListType
RMAX = bass.bass_isa.ReduceOp.max

P = 128
D = 512
KT = D // P
I = 1536
IT = I // P
H = 16
DH = D // H
HG = P // DH
TOK = 256
T = TOK // P
EPS = 1e-5
P_SHIFT = 20
EXPONENT = 0x7F800000
E4M3_TINY = 2.0 ** -6
E4M3_MAGIC = 1.5 * 2.0 ** 20
SQUARE = 0.55
SQUARE_FLOOR = 3 * D * 2.0 ** -14


def sandwich(nc, x, w_qkv_t, b_qk, b_v, w_out_t, b_out, gate_w, up_w, down_w, gate_s, up_s, down_s,
             mask_c, decay_q_c, decay_k_c, lam_c, eye_c, out):
    units = x.shape[0] // TOK
    per_seq = 1024 // TOK
    x_u = x.rearrange("(n t p) d -> n p t d", t=T, p=P)
    out_u = out.rearrange("(n t p) d -> n t p d", t=T, p=P)

    with ExitStack() as ctx:
        def sb(name, shape, dt=F32):
            return ctx.enter_context(nc.sbuf_tensor(name, shape, dt))

        def sem(name):
            return ctx.enter_context(nc.semaphore(name))

        wqkv_hi = sb("wqkv_hi", [P, KT, 3 * D], F16)
        wqkv_lo = sb("wqkv_lo", [P, KT, 3 * D], F16)
        wout_hl = sb("wout_hl", [P, 2, KT, D], F16)
        gate_q = sb("gate_q", [P, KT, I], F16)
        up_q = sb("up_q", [P, KT, I], F16)
        down_q = sb("down_q", [P, IT, D], F16)
        mask = sb("mask", [P, H, P])
        decay_q = sb("decay_q", [P, D])
        decay_k = sb("decay_k", [P, D])
        lam = sb("lam", [P, KT, P])
        eye = sb("eye", [P, P])
        bqk = sb("bqk", [P, 2 * KT])
        bv = sb("bv", [P, D])
        bo = sb("bo", [P, D])
        ds_t = sb("ds_t", [P, D])
        gs_t = sb("gs_t", [P, IT])
        us_t = sb("us_t", [P, IT])
        small = sb("small", [P, 64])
        eps_t = sb("eps_t", [P, 2, T])
        ones = sb("ones", [P, P], F16)

        x_t = sb("x_t", [P, 2, T, D])
        nrm = sb("nrm", [P, T, D])
        x_hl = sb("x_hl", [P, 2, KT, TOK], F16)
        qk = sb("qk", [P, 2 * KT, TOK])
        v32 = sb("v32", [P, T, D])
        v_hl = sb("v_hl", [P, T, H, 2, DH], F16)
        kd = sb("kd", [P, T, D])
        p32 = sb("p32", [P, 2, D])
        o32 = sb("o32", [P, T, D])
        o_t = sb("o_t", [P, T, 2, KT, P], F16)
        o_scale = sb("o_scale", [P, 5, T])
        y32 = sb("y32", [P, T, D])
        state = sb("state", [P, KT, P])
        state_d = sb("state_d", [P, KT, P])
        x1 = sb("x1", [P, 2, T, D])
        stats = sb("stats", [P, 4, T, 6])
        mv = sb("mv", [P, 4, T, 2])
        rstd = sb("rstd", [P, 4, 2, T])

        att_pool = sb("att_pool", [P, KT * 3 * D])
        stacks = att_pool[:, 0:2 * H * TOK // 2].bitcast(F16).rearrange(
            "p (s h t) -> p s h t", s=2, h=H)
        split = att_pool[:, 2 * H * TOK // 2:KT * 3 * D].bitcast(F16)
        qk_hl = split.rearrange("p (s k t) -> p s k t", s=2, k=2 * KT)
        pr_hl = split.rearrange("p (s h c) -> p s h c", s=2, h=H)
        w_stage = att_pool[:, :].rearrange("p (k n) -> p k n", k=KT)
        ffn_pool = sb("ffn_pool", [P, 7680])
        h_hl = ffn_pool[:, 0:3072].bitcast(F16).rearrange("p (s k t) -> p s k t", s=2, k=IT)
        sil = ffn_pool[:, 3072:3584].rearrange("p (j t) -> p j t", j=2)
        y2 = ffn_pool[:, 3584:4608].rearrange("p (t d) -> p t d", t=T)
        h32 = ffn_pool[:, 4608:5632].rearrange("p (i n) -> p i n", i=2)
        x1_hl = ffn_pool[:, 5632:6656].bitcast(F16).rearrange("p (s k t) -> p s k t", s=2, k=KT)
        f_stage = [ffn_pool[:, n * I:(n + 1) * I] for n in range(3)]
        f_magic = [ffn_pool[:, n * I:(n + 1) * I] for n in (3, 4)]

        wout_stage = x1[:, :].rearrange("p u t d -> p (u t) d")

        bank = [ctx.enter_context(nc.psum_tensor(f"bank{n}", [P, D], F32)) for n in range(8)]
        b_gate, b_up, b_y, b_att = bank[0], bank[1], bank[2], bank[7]
        b_t = [bank[3], bank[4]]
        b_s = [bank[5], bank[6]]

        w_in = [sem(f"w_in{k}") for k in range(KT)]
        bias_in, tab_in, scl_in, wout_in = sem("bias_in"), sem("tab_in"), sem("scl_in"), sem("wout_in")
        f_in = [sem(f"f_in{n}") for n in range(3)]
        chain = sem("chain")
        w_max, w_max_all = sem("w_max"), sem("w_max_all")
        w_hi_d, w_lo_d = sem("w_hi_d"), sem("w_lo_d")
        square_d, square_mm, root_d = sem("square_d"), sem("square_mm"), sem("root_d")
        f_magic_d, f_sum_d, f_q_d = sem("f_magic_d"), sem("f_sum_d"), sem("f_q_d")
        eye_in, w_scale_d = sem("eye_in"), sem("w_scale_d")
        norms_d = sem("norms_d")
        wout_max, wout_max_all, wout_scale_d = sem("wout_max"), sem("wout_max_all"), sem("wout_scale_d")
        wout_hi_d, wout_lo_d = sem("wout_hi_d"), sem("wout_lo_d")
        bn_seen = sem("bn_seen")
        state_0, eps_d = sem("state_0"), sem("eps_d")
        x_in = [sem("x_in0"), sem("x_in1")]
        y2_free = sem("y2_free")
        q_stacked, k_stacked, stored = sem("q_stacked"), sem("k_stacked"), sem("stored")
        x_tr, qk_mm, v_mm, x1_tr, k_tr = sem("x_tr"), sem("qk_mm"), sem("v_mm"), sem("x1_tr"), sem("k_tr")
        score_mm, carry_mm, state_mm, att_mm = sem("score_mm"), sem("carry_mm"), sem("state_mm"), sem("att_mm")
        o_tr, out_mm, gate_mm, up_mm, down_mm = sem("o_tr"), sem("out_mm"), sem("gate_mm"), sem("up_mm"), sem("down_mm")
        x_hi_d, qk_d, qk_hi_d, v_hi_d, x1_hi_d = sem("x_hi_d"), sem("qk_d"), sem("qk_hi_d"), sem("v_hi_d"), sem("x1_hi_d")
        p_hi_d, o_t_d, silu_d, h_hi_d = sem("p_hi_d"), sem("o_t_d"), sem("silu_d"), sem("h_hi_d")
        x_lo_d, v_d, kd_d, x1_lo_d = sem("x_lo_d"), sem("v_d"), sem("kd_d"), sem("x1_lo_d")
        p_d, carry_d, state_u, o_d, h_d, y_d, y2_d = (sem("p_d"), sem("carry_d"), sem("state_u"), sem("o_d"),
                                                      sem("h_d"), sem("y_d"), sem("y2_d"))
        o_half_d = sem("o_half_d")
        o_max_d, o_exp_d, o_div_d, o_mul_d, o_scaled_d, o_lo_d = (
            sem("o_max_d"), sem("o_exp_d"), sem("o_div_d"), sem("o_mul_d"), sem("o_scaled_d"), sem("o_lo_d"))
        bn_d = [sem(f"bn_d{n}") for n in range(4)]
        mv_d = [sem(f"mv_d{n}") for n in range(4)]
        nrm_d = [sem(f"nrm_d{n}") for n in range(4)]
        qk_lo_d, v_lo_d, p_lo_d, h_lo_d = sem("qk_lo_d"), sem("v_lo_d"), sem("p_lo_d"), sem("h_lo_d")
        state_dec, x1_d, fin_d = sem("state_dec"), sem("x1_d"), sem("fin_d")
        ve_d = [sem(f"ve_d{n}") for n in range(4)]
        rs_d = [sem(f"rs_d{n}") for n in range(4)]

        N_BIAS, N_TAB, N_SCL = 2, 4, 3
        LN_X, LN_Y, LN_X1, LN_Y2 = range(4)
        last = units - 1

        def piece_in(n):
            w, k = (gate_w, up_w, down_w)[n // 4], n % 4
            if n < 8:
                return w[k * P:(k + 1) * P, :]
            return w[3 * k * P:3 * (k + 1) * P, :].rearrange("(c p) n -> p c n", p=P)

        def stage_for(n):
            return f_stage[n % 3] if n < 8 else f_stage[n % 3].rearrange("p (c n) -> p c n", n=D)

        def piece_out(n):
            if n < 8:
                return (gate_q, up_q)[n // 4][:, n % 4]
            return down_q[:, 3 * (n % 4):3 * (n % 4) + 3].rearrange("p c n -> p (c n)")

        def slots(fori, slot, start, end):
            start()
            slot(1, 1, att=True, nxt=True)
            with fori(0, (units - per_seq) // per_seq) as seq:
                for j in range(2, per_seq + 2):
                    slot(seq * per_seq + j, j % per_seq, att=True, nxt=True)
            for s in range(units - per_seq + 2, units + 1):
                slot(s, s % per_seq, att=s < units, nxt=s < last)
            end()

        def early(s):
            return type(s) is int and s == 1

        def squares(n):
            buf = f_stage[n % 3] if n >= 9 else y32[:, :].rearrange("p t d -> p (t d)")
            return buf.bitcast(F16)[:, 0:I]

        def att_out(half):
            return (b_att, b_y)[half][:, :].rearrange("p (h s d) -> p h s d", s=2, d=DH)

        def heads(s, g):
            return slice(g, H, HG) if type(s) is int and s == 0 else slice(HG * g, HG * (g + 1))

        def by_head(half):
            return half.rearrange("p (h c) -> p h c", h=HG)

        block = ctx.enter_context(nc.Block())

        @block.sync
        def _(sp):
            def start():
                sp.sem_inc(y2_free, 1)
                sp.dma_start(x_t[:, 0], x_u[0]).then_inc(x_in[0], 16)
                for k in range(KT):
                    sp.dma_start(w_stage[:, k], w_qkv_t[k * P:(k + 1) * P, :]).then_inc(w_in[k], 16)
                for n in range(3):
                    sp.dma_start(stage_for(n), piece_in(n)).then_inc(f_in[n], 16)
                for dst, src in ((mask[:, :, :], mask_c), (decay_q[:, :], decay_q_c),
                                 (decay_k[:, :], decay_k_c), (lam[:, :, :], lam_c)):
                    sp.dma_start(dst, src).then_inc(tab_in, 16)
                sp.dma_start(wout_stage, w_out_t.rearrange("(k p) n -> p k n", p=P)).then_inc(wout_in, 16)
                sp.dma_start(bo[:, :], b_out).then_inc(wout_in, 16)
                sp.dma_start(x_t[:, 1], x_u[1]).then_inc(x_in[1], 16)
                for n in range(3, 12):
                    sp.wait_ge(f_q_d, n - 2)
                    sp.dma_start(stage_for(n), piece_in(n)).then_inc(f_in[n % 3], 16)
                stack(1)

            def stack(n):
                for which, done, parts in ((0, q_stacked, (0, 1, 0, 1)), (1, k_stacked, (0, 0, 1, 1))):
                    sp.wait_ge(qk_hi_d, 4 * n - 2 + 2 * which)
                    sp.wait_ge(qk_lo_d, 4 * n - 2 + 2 * which)
                    for j in range(HG):
                        for r in range(4):
                            sp.dma_start(stacks[DH * r:DH * (r + 1), which, j::HG, :],
                                         qk_hl[DH * j:DH * (j + 1), parts[r], KT * which:KT * (which + 1), :]
                                         ).then_inc(done, 16)

            def store(v, t):
                sp.wait_ge(fin_d, 2 * v + t + 1)
                sp.dma_start(out_u[v, t], y2[:, t]).then_inc(stored, 16)

            def store_last(v):
                store(v, T - 1)
                sp.wait_ge(stored, 16 * T * v + 16 * T)
                sp.sem_inc(y2_free, 1)

            def slot(s, m, att, nxt):
                if nxt:
                    sp.wait_ge(x1_d, 2 * s)
                    sp.dma_start(x_t[:, (m + 1) % 2], x_u[s + 1]).then_inc(x_in[(m + 1) % 2], 16)
                if not early(s):
                    store_last(s - 2)
                if nxt:
                    stack(s + 1)
                store(s - 1, 0)

            slots(sp.Fori, slot, start, lambda: store_last(last))

        @block.scalar
        def _(act):
            def start():
                act.dma_start(eye[:, :], eye_c).then_inc(eye_in, 16)
                act.dma_start(bqk[:, :], b_qk).then_inc(bias_in, 16)
                act.dma_start(bv[:, :], b_v).then_inc(bias_in, 16)
                act.dma_start(gs_t[:, :], gate_s).then_inc(scl_in, 16)
                act.dma_start(us_t[:, :], up_s).then_inc(scl_in, 16)
                act.dma_start(ds_t[:, :], down_s).then_inc(scl_in, 16)
                split_x(0)
                act.wait_ge(w_scale_d, 1)
                for k in range(KT):
                    w_hi(wqkv_hi[:, k, 0:2 * D], w_stage[:, k, 0:2 * D])
                w_hi(wqkv_hi[:, :, 2 * D:3 * D], w_stage[:, :, 2 * D:3 * D])
                for i in range(4):
                    front(0, i)
                square(0)
                square(1)
                v_hi(0)
                square(2)
                probs_hi(0, 0, 0)
                square(3)
                probs_hi(0, 0, 1)
                act.wait_ge(wout_scale_d, 1)
                nc.scalar.activation(wout_hl[:, 0], wout_stage, ACT.Copy, scale=small[:, 18:19]
                                     ).then_inc(wout_hi_d, 1)
                square(4)
                probs_hi(0, 1, 0)
                square(5)
                probs_hi(0, 1, 1)
                split_x(1)
                square(6)
                front(1, 0)
                front(1, 1)
                square(7)
                front(1, 2)
                front(1, 3)
                square(8)
                out_t(0, 0)
                out_t(0, 1)
                square(9)
                v_hi(1)
                square(10)
                square(11)

            def w_hi(dst, src):
                nc.scalar.activation(dst, src, ACT.Copy, scale=small[:, 11:12]).then_inc(w_hi_d, 1)

            def square(n):
                act.wait_ge(f_q_d, n + 1)
                if 1 <= n <= 8:
                    act.wait_ge(square_mm, n)
                nc.scalar.activation(squares(n), piece_out(n), ACT.Square, scale=SQUARE).then_inc(square_d, 1)

            def front(n, i):
                act.wait_ge(qk_mm, 4 * n + i + 1)
                for j in range(2):
                    o = 2 * i + j
                    ins = nc.scalar.activation(qk[:, o], b_t[i % 2][:, j * TOK:(j + 1) * TOK],
                                               ACT.Identity, bias=bqk[:, o:o + 1])
                ins.then_inc(qk_d, 1)
                if not (type(n) is int and n == 0):
                    act.wait_ge(qk_d, 4 * n + i + 1)
                    nc.scalar.copy(qk_hl[:, 0, 2 * i:2 * i + 2].rearrange("p k t -> p (k t)"),
                                   qk[:, 2 * i:2 * i + 2].rearrange("p k t -> p (k t)")).then_inc(qk_hi_d, 1)

            def v_hi(n):
                for t in range(T):
                    act.wait_ge(v_d, 2 * n + t + 1)
                    nc.scalar.copy(v_hl[:, t, :, 0], v32[:, t].rearrange("p (h d) -> p h d", h=H)
                                   ).then_inc(v_hi_d, 1)

            def split_x(n):
                for j in range(2):
                    act.wait_ge(x_tr, 2 * n + j + 1)
                    nc.scalar.copy(x_hl[:, 0, 2 * j:2 * j + 2].rearrange("p k t -> p (k t)"),
                                   b_s[j][:, :]).then_inc(x_hi_d, 1)

            def probs_hi(s, c, half):
                if c and half == 0:
                    act.wait_ge(att_mm, 2 * s + 1)
                for g in range(2 * half, 2 * half + 2):
                    act.wait_ge(p_d, 8 * s + 4 * c + g + 1)
                    nc.scalar.copy(pr_hl[:, 0, heads(s, g)], by_head(p32[:, g % 2])).then_inc(p_hi_d, 1)

            def silu(v, i):
                act.wait_ge(gate_mm, 6 * v + i + 1)
                if i:
                    act.wait_ge(h_d, 6 * v + i)
                for j in range(2):
                    ins = nc.scalar.activation(sil[:, j], b_gate[:, j * TOK:(j + 1) * TOK], ACT.Silu,
                                               scale=gs_t[:, 2 * i + j:2 * i + j + 1])
                ins.then_inc(silu_d, 1)

            def h_hi(v, i):
                act.wait_ge(h_d, 6 * v + i + 1)
                nc.scalar.copy(h_hl[:, 0, 2 * i:2 * i + 2].rearrange("p k t -> p (k t)"),
                               h32[:, i % 2]).then_inc(h_hi_d, 1)

            def out_t(s, c):
                act.wait_ge(o_tr, 2 * s + c + 1)
                nc.scalar.copy(o_t[:, c, 0].rearrange("p k c -> p (k c)"), b_s[c][:, :]).then_inc(o_t_d, 1)

            def slot(s, m, att, nxt):
                v = s - 1
                for j in range(2):
                    act.wait_ge(x1_tr, 2 * v + j + 1)
                    nc.scalar.copy(x1_hl[:, 0, 2 * j:2 * j + 2].rearrange("p k t -> p (k t)"),
                                   (b_y, b_att)[j][:, :]).then_inc(x1_hi_d, 1)
                if att:
                    probs_hi(s, 0, 0)
                silu(v, 0)
                if att:
                    probs_hi(s, 0, 1)
                silu(v, 1)
                h_hi(v, 0)
                silu(v, 2)
                h_hi(v, 1)
                if att:
                    probs_hi(s, 1, 0)
                silu(v, 3)
                h_hi(v, 2)
                if att:
                    probs_hi(s, 1, 1)
                silu(v, 4)
                if nxt:
                    split_x(s + 1)
                h_hi(v, 3)
                silu(v, 5)
                h_hi(v, 4)
                h_hi(v, 5)
                if nxt:
                    front(s + 1, 0)
                    front(s + 1, 1)
                if att:
                    out_t(s, 0)
                    out_t(s, 1)
                if nxt:
                    front(s + 1, 2)
                    front(s + 1, 3)
                    v_hi(s + 1)

            slots(act.Fori, slot, start, lambda: None)

        @block.tensor
        def _(pe):
            def transpose_x(n):
                pe.wait_ge(nrm_d[LN_X], 2 * n + 2)
                for j in range(2):
                    for kk in range(2):
                        for t in range(T):
                            ins = nc.tensor.transpose(b_s[j][:, kk * TOK + t * P:kk * TOK + (t + 1) * P],
                                                      nrm[:, t, (2 * j + kk) * P:(2 * j + kk + 1) * P], eye[:, :])
                    ins.then_inc(x_tr, 1)

            def start():
                pe.wait_ge(eye_in, 16)
                transpose_x(0)
                for i in range(4):
                    project_qk(0, i)
                project_v(0)
                sum_squares(0)
                sum_squares(1)
                transpose_k(0)
                pe.wait_ge(state_0, 1)
                scores(0, 0, 0)
                carry_and_state(0, 0)
                scores(0, 0, 1)
                sum_squares(2)
                attend(0, 0)
                sum_squares(3)
                scores(0, 1, 0)
                scores(0, 1, 1)
                sum_squares(4)
                carry_and_state(0, 1)
                pe.wait_ge(p_d, 8)
                transpose_x(1)
                sum_squares(5)
                attend(0, 1)
                project_qk(1, 0)
                project_qk(1, 1)
                sum_squares(6)
                project_qk(1, 2)
                project_qk(1, 3)
                sum_squares(7)
                transpose_o(0, 0, True)
                transpose_o(0, 1, True)
                sum_squares(8)
                pe.wait_ge(wout_lo_d, 1)
                project(0, 0)
                project(0, 1)
                project_v(1)
                sum_squares(9)
                transpose_k(1)
                sum_squares(10)
                sum_squares(11)

            def sum_squares(n):
                pe.wait_ge(square_d, n + 1)
                if n == 0:
                    pe.wait_ge(eps_d, 3)
                if n == 8:
                    pe.wait_ge(norms_d, 1)
                for k in range(3):
                    ins = nc.tensor.matmul((b_gate, b_up)[n // 4 % 2][:, :], ones[:, :], squares(n)[:, k * D:(k + 1) * D],
                                           start=(n % 4 == 0 and k == 0), stop=(n % 4 == 3 and k == 2))
                ins.then_inc(square_mm, 1)

            def gate_up(v, i):
                if i == 0:
                    pe.wait_ge(x1_lo_d, 2 * v + 2)
                else:
                    pe.wait_ge(silu_d, 6 * v + i)
                for w, b, done in ((gate_q, b_gate, gate_mm), (up_q, b_up, up_mm)):
                    if done is up_mm and i:
                        pe.wait_ge(h_d, 6 * v + i)
                    for j in range(2):
                        o = 2 * i + j
                        for k in range(KT):
                            for part in range(2):
                                ins = nc.tensor.matmul(b[:, j * TOK:(j + 1) * TOK], w[:, k, o * P:(o + 1) * P],
                                                       x1_hl[:, part, k], start=(k == 0 and part == 0),
                                                       stop=(k == KT - 1 and part == 1))
                    ins.then_inc(done, 1)

            def down(v, t):
                if t == 0:
                    pe.wait_ge(h_d, 6 * v + 6)
                    pe.wait_ge(h_lo_d, 6 * v + 5)
                for k in range(IT):
                    if t == 0 and k == IT - 2:
                        pe.wait_ge(h_hi_d, 6 * v + 6)
                        pe.wait_ge(h_lo_d, 6 * v + 6)
                    for part in range(2):
                        ins = nc.tensor.matmul((b_gate, b_up)[t][:, :], h_hl[:, part, k, t * P:(t + 1) * P],
                                               down_q[:, k], start=(k == 0 and part == 0),
                                               stop=(k == IT - 1 and part == 1))
                ins.then_inc(down_mm, 1)

            def scores(s, c, half):
                first = type(s) is int and s == 0
                if c == 0 and half == 0 and not first:
                    pe.wait_ge(q_stacked, 256 * s)
                    pe.wait_ge(k_stacked, 256 * s)
                    pe.wait_ge(o_lo_d, 2 * s)
                for g in range(2 * half, 2 * half + 2):
                    if c or half:
                        pe.wait_ge(p_d, 8 * s + 4 * c + g - 1)
                    for j in range(HG):
                        if first:
                            k_t = qk[DH * g:DH * (g + 1), KT + j, c * P:(c + 1) * P]
                            q_t = qk[DH * g:DH * (g + 1), j, c * P:(c + 1) * P]
                        else:
                            k_t = stacks[:, 1, HG * g + j, c * P:(c + 1) * P]
                            q_t = stacks[:, 0, HG * g + j, c * P:(c + 1) * P]
                        ins = nc.tensor.matmul(b_s[g % 2][:, j * P:(j + 1) * P], k_t, q_t,
                                               start=True, stop=True)
                    ins.then_inc(score_mm, 1)

            def carry_and_state(s, c):
                if c == 0:
                    pe.wait_ge(kd_d, 2 * s + 2)
                else:
                    pe.wait_ge(carry_d, 2 * s + 1)
                if not (c == 0 and type(s) is int and s == 0):
                    pe.wait_ge(state_u, 2 * s + c)
                for g in range(KT):
                    ins = nc.tensor.matmul(b_t[0][:, g * P:(g + 1) * P], qk[:, g, c * P:(c + 1) * P],
                                           state[:, g], start=True, stop=True)
                ins.then_inc(carry_mm, 1)
                for g in range(KT):
                    ins = nc.tensor.matmul(b_t[1][:, g * P:(g + 1) * P], kd[:, c, g * P:(g + 1) * P],
                                           v32[:, c, g * P:(g + 1) * P], start=True, stop=True)
                ins.then_inc(state_mm, 1)

            def attend(s, c):
                pe.wait_ge(p_hi_d, 8 * s + 4 * c + 4)
                pe.wait_ge(p_lo_d, 8 * s + 4 * c + 4)
                pe.wait_ge(v_hi_d, 2 * s + c + 1)
                pe.wait_ge(v_lo_d, 2 * s + c + 1)
                if c:
                    pe.wait_ge(o_d, 2 * s + 1)
                for h in range(H):
                    out_h = att_out(h // (H // 2))[:, h % (H // 2)]
                    nc.tensor.matmul(out_h.rearrange("p s d -> p (s d)"), pr_hl[:, 0, h],
                                     v_hl[:, c, h].rearrange("p s d -> p (s d)"), start=True, stop=False)
                    ins = nc.tensor.matmul(out_h[:, 0], pr_hl[:, 1, h], v_hl[:, c, h, 0], start=False, stop=True)
                ins.then_inc(att_mm, 1)

            def transpose_o(s, c, nxt):
                pe.wait_ge(o_scaled_d, 2 * s + c + 1)
                if nxt:
                    pe.wait_ge(x_lo_d, 2 * s + 4)
                elif c == 0:
                    pe.wait_ge(p_d, 8 * s + 8)
                for k in range(KT):
                    ins = nc.tensor.transpose(b_s[c][:, k * P:(k + 1) * P], o32[:, c, k * P:(k + 1) * P], eye[:, :])
                ins.then_inc(o_tr, 1)

            def project(s, c):
                pe.wait_ge(o_lo_d, 2 * s + c + 1)
                for k in range(KT):
                    for n, (a, b) in enumerate(((0, 0), (0, 1), (1, 0))):
                        ins = nc.tensor.matmul((b_y, b_att)[c][:, :], o_t[:, c, a, k], wout_hl[:, b, k],
                                               start=(k == 0 and n == 0), stop=(k == KT - 1 and n == 2))
                ins.then_inc(out_mm, 1)

            def project_qk(n, i):
                first = type(n) is int and n == 0
                pe.wait_ge(x_lo_d, 2 * n + 2)
                if i >= 2:
                    pe.wait_ge(qk_d, 4 * n + i - 1)
                elif not first:
                    pe.wait_ge((carry_d, state_u)[i], 2 * n)
                for j in range(2):
                    o = 2 * i + j
                    for k in range(KT):
                        if first and i == 0 and j == 0:
                            pe.wait_ge(w_hi_d, k + 1)
                            pe.wait_ge(w_lo_d, k + 1)
                        for q, (a, b) in enumerate(((0, 0), (0, 1), (1, 0))):
                            ins = nc.tensor.matmul(b_t[i % 2][:, j * TOK:(j + 1) * TOK],
                                                   (wqkv_hi, wqkv_lo)[a][:, k, o * P:(o + 1) * P],
                                                   x_hl[:, b, k], start=(k == 0 and q == 0),
                                                   stop=(k == KT - 1 and q == 2))
                ins.then_inc(qk_mm, 1)

            def project_v(n):
                if type(n) is int and n == 0:
                    pe.wait_ge(w_hi_d, KT + 1)
                    pe.wait_ge(w_lo_d, KT + 1)
                for t in range(T):
                    pe.wait_ge(qk_d, 4 * n + 3 + t)
                    for k in range(KT):
                        for q, (a, b) in enumerate(((0, 0), (0, 1), (1, 0))):
                            ins = nc.tensor.matmul(b_t[t][:, :], x_hl[:, b, k, t * P:(t + 1) * P],
                                                   (wqkv_hi, wqkv_lo)[a][:, k, 2 * D:3 * D],
                                                   start=(k == 0 and q == 0), stop=(k == KT - 1 and q == 2))
                    ins.then_inc(v_mm, 1)

            def transpose_k(n):
                for c in range(T):
                    pe.wait_ge(v_d, 2 * n + c + 1)
                    for g in range(KT):
                        ins = nc.tensor.transpose(b_t[c][:, g * P:(g + 1) * P],
                                                  qk[:, KT + g, c * P:(c + 1) * P], eye[:, :])
                    ins.then_inc(k_tr, 1)

            def slot(s, m, att, nxt):
                v = s - 1
                pe.wait_ge(nrm_d[LN_X1], 2 * v + 2)
                for j in range(2):
                    for kk in range(2):
                        for t in range(T):
                            ins = nc.tensor.transpose((b_y, b_att)[j][:, kk * TOK + t * P:kk * TOK + (t + 1) * P],
                                                      nrm[:, t, (2 * j + kk) * P:(2 * j + kk + 1) * P], eye[:, :])
                    ins.then_inc(x1_tr, 1)
                if att:
                    scores(s, 0, 0)
                    carry_and_state(s, 0)
                gate_up(v, 0)
                if att:
                    scores(s, 0, 1)
                gate_up(v, 1)
                gate_up(v, 2)
                if att:
                    attend(s, 0)
                    scores(s, 1, 0)
                gate_up(v, 3)
                if att:
                    scores(s, 1, 1)
                    carry_and_state(s, 1)
                gate_up(v, 4)
                if nxt:
                    pe.wait_ge(p_d, 8 * s + 8)
                    transpose_x(s + 1)
                if att and not nxt:
                    attend(s, 1)
                gate_up(v, 5)
                if att and nxt:
                    attend(s, 1)
                if nxt:
                    project_qk(s + 1, 0)
                    project_qk(s + 1, 1)
                if att:
                    transpose_o(s, 0, nxt)
                    transpose_o(s, 1, nxt)
                if nxt:
                    project_qk(s + 1, 2)
                    project_qk(s + 1, 3)
                if att:
                    project(s, 0)
                if att and not nxt:
                    project(s, 1)
                down(v, 0)
                if att and nxt:
                    project(s, 1)
                if nxt:
                    project_v(s + 1)
                down(v, 1)
                if nxt:
                    transpose_k(s + 1)

            slots(pe.Fori, slot, start, lambda: None)

        @block.gpsimd
        def _(pool):
            def inverse_std(ln, val, cols):
                nc.gpsimd.tensor_tensor(rstd[:, ln, 0, cols], mv[:, ln, cols, 1], eps_t[:, 0, cols],
                                        ALU.add).then_inc(ve_d[ln], 1)
                pool.wait_ge(ve_d[ln], val)
                nc.gpsimd.tensor_tensor(rstd[:, ln, 1, cols], rstd[:, ln, 0, cols], eps_t[:, 1, cols],
                                        ALU.pow).then_inc(rs_d[ln], 1)

            def inverse_std_x(n):
                pool.wait_ge(mv_d[LN_X], 2 * n + 2)
                inverse_std(LN_X, n + 1, slice(0, T))

            def start():
                nc.gpsimd.memset(eps_t[:, 0, :], EPS).then_inc(eps_d, 1)
                nc.gpsimd.memset(eps_t[:, 1, :], -0.5).then_inc(eps_d, 1)
                nc.gpsimd.memset(ones[:, :], 1.0).then_inc(eps_d, 1)
                nc.gpsimd.memset(state[:, :, :], 0.0).then_inc(state_0, 1)
                pool.wait_ge(eps_d, 3)
                inverse_std_x(0)
                pool.wait_ge(w_max, 1)
                nc.gpsimd.partition_all_reduce(small[:, 6:7], small[:, 5:6], P, RMAX).then_inc(w_max_all, 1)
                pool.wait_ge(state_0, 1)
                quant_sum(0)
                quant_sum(1)
                quant_sum(2)
                quant_sum(3)
                v_lo(0)
                quant_sum(4)
                pool.wait_ge(wout_max, 1)
                nc.gpsimd.partition_all_reduce(small[:, 36:39], small[:, 20:23], P, RMAX).then_inc(wout_max_all, 1)
                pool.wait_ge(tab_in, 16 * N_TAB)
                state_decay(0, 0)
                probs_lo(0, 0, 0)
                quant_sum(5)
                probs_lo(0, 0, 1)
                quant_sum(6)
                inverse_std_x(1)
                state_decay(0, 1)
                probs_lo(0, 1, 0)
                quant_sum(7)
                probs_lo(0, 1, 1)
                quant_sum(8)
                quant_sum(9)
                qk_lo(1, 0)
                qk_lo(1, 1)
                quant_sum(10)
                qk_lo(1, 2)
                qk_lo(1, 3)
                quant_sum(11)
                pool.wait_ge(norms_d, 2)
                nc.gpsimd.tensor_tensor(small[:, 51:52], small[:, 50:51], eps_t[:, 1, 0:1], ALU.pow).then_inc(root_d, 1)
                y_inverse_std(0, 0)
                y_inverse_std(0, 1)
                residual(0, 0, 0)
                residual(0, 0, 1)
                x1_inverse_std(0, 0)
                x1_inverse_std(0, 1)
                v_lo(1)

            def quant_sum(n):
                pool.wait_ge(f_magic_d, n + 1)
                nc.gpsimd.tensor_tensor(f_stage[n % 3], f_stage[n % 3], f_magic[n % 2], ALU.add
                                        ).then_inc(f_sum_d, 1)

            def h_lo(v, i):
                pool.wait_ge(h_hi_d, 6 * v + i + 1)
                nc.gpsimd.tensor_tensor(h_hl[:, 1, 2 * i:2 * i + 2].rearrange("p k t -> p (k t)"), h32[:, i % 2],
                                        h_hl[:, 0, 2 * i:2 * i + 2].rearrange("p k t -> p (k t)"),
                                        ALU.subtract).then_inc(h_lo_d, 1)

            def state_decay(s, c):
                if not (c == 0 and type(s) is int and s == 0):
                    pool.wait_ge(state_u, 2 * s + c)
                nc.gpsimd.tensor_tensor(state_d[:, :, :], state[:, :, :], lam[:, :, :], ALU.mult
                                        ).then_inc(state_dec, 1)

            def probs_lo(s, c, half):
                for g in range(2 * half, 2 * half + 2):
                    pool.wait_ge(p_hi_d, 8 * s + 4 * c + g + 1)
                    nc.gpsimd.tensor_tensor(pr_hl[:, 1, heads(s, g)], by_head(p32[:, g % 2]),
                                            pr_hl[:, 0, heads(s, g)], ALU.subtract).then_inc(p_lo_d, 1)

            def qk_lo(n, i):
                pool.wait_ge(qk_hi_d, 4 * n + i - 3)
                nc.gpsimd.tensor_tensor(qk_hl[:, 1, 2 * i:2 * i + 2].rearrange("p k t -> p (k t)"),
                                        qk[:, 2 * i:2 * i + 2].rearrange("p k t -> p (k t)"),
                                        qk_hl[:, 0, 2 * i:2 * i + 2].rearrange("p k t -> p (k t)"),
                                        ALU.subtract).then_inc(qk_lo_d, 1)

            def v_lo(n):
                for t in range(T):
                    pool.wait_ge(v_hi_d, 2 * n + t + 1)
                    nc.gpsimd.tensor_tensor(v_hl[:, t, :, 1], v32[:, t].rearrange("p (h d) -> p h d", h=H),
                                            v_hl[:, t, :, 0], ALU.subtract).then_inc(v_lo_d, 1)

            def y_inverse_std(s, t):
                pool.wait_ge(mv_d[LN_Y], 2 * s + t + 1)
                inverse_std(LN_Y, 2 * s + t + 1, slice(t, t + 1))

            def residual(s, m, t):
                pool.wait_ge(nrm_d[LN_Y], 2 * s + t + 1)
                nc.gpsimd.tensor_tensor(x1[:, m % 2, t], x_t[:, m % 2, t], y32[:, t], ALU.add).then_inc(x1_d, 1)

            def x1_inverse_std(s, t):
                pool.wait_ge(mv_d[LN_X1], 2 * s + t + 1)
                inverse_std(LN_X1, 2 * s + t + 1, slice(t, t + 1))

            def y2_inverse_std(v, t):
                pool.wait_ge(mv_d[LN_Y2], 2 * v + t + 1)
                inverse_std(LN_Y2, 2 * v + t + 1, slice(t, t + 1))

            def final(v, par, t):
                pool.wait_ge(nrm_d[LN_Y2], 2 * v + t + 1)
                nc.gpsimd.tensor_tensor(y2[:, t], x1[:, par, t], y2[:, t], ALU.add).then_inc(fin_d, 1)

            def slot(s, m, att, nxt):
                v = s - 1
                if att:
                    state_decay(s, 0)
                    probs_lo(s, 0, 0)
                if not early(s):
                    y2_inverse_std(s - 2, 1)
                if att:
                    probs_lo(s, 0, 1)
                if not early(s):
                    final(s - 2, m % 2, 1)
                for i in range(2):
                    h_lo(v, i)
                if nxt:
                    inverse_std_x(s + 1)
                if att:
                    state_decay(s, 1)
                h_lo(v, 2)
                if att:
                    probs_lo(s, 1, 0)
                    probs_lo(s, 1, 1)
                for i in range(3, 6):
                    h_lo(v, i)
                if nxt:
                    for i in range(4):
                        qk_lo(s + 1, i)
                if att and not nxt:
                    for t in range(T):
                        y_inverse_std(s, t)
                    for t in range(T):
                        residual(s, m, t)
                        x1_inverse_std(s, t)
                for t in range(T):
                    if att and nxt:
                        y_inverse_std(s, t)
                        residual(s, m, t)
                        x1_inverse_std(s, t)
                    if t == 0:
                        y2_inverse_std(v, 0)
                        final(v, (m + 1) % 2, 0)
                if nxt:
                    v_lo(s + 1)

            def end():
                y2_inverse_std(last, 1)
                final(last, last % 2, 1)

            slots(pool.Fori, slot, start, end)

        @block.vector
        def _(dve):
            links = [0]

            def link(ins):
                links[0] += 1
                ins.then_inc(chain, 1)
                dve.wait_ge(chain, links[0])

            def col(a, n=1):
                return small[:, a:a + n]

            def power_of_two(dst, src, low, high):
                link(nc.vector.tensor_scalar(dst.bitcast(U32), src.bitcast(U32), EXPONENT, None, ALU.bitwise_and))
                link(nc.vector.tensor_scalar(dst, dst, low, high, ALU.max, ALU.min))

            def prepare_qkv():
                for k in range(KT):
                    dve.wait_ge(w_in[k], 16)
                    nc.vector.tensor_reduce(col(k), w_stage[:, k], AX.X, ALU.max, apply_absolute_value=True)
                dve.wait_ge(bias_in, 16 * N_BIAS)
                nc.vector.tensor_reduce(col(7), bqk[:, :], AX.X, ALU.max, apply_absolute_value=True)
                link(nc.vector.tensor_reduce(col(8), bv[:, :], AX.X, ALU.max, apply_absolute_value=True))
                link(nc.vector.tensor_tensor(col(7), col(7), col(8), ALU.max))
                link(nc.vector.tensor_scalar(col(4), col(7), 1.0 / 256.0, None, ALU.mult))
                nc.vector.tensor_reduce(col(5), col(0, 5), AX.X, ALU.max).then_inc(w_max, 1)
                dve.wait_ge(w_max_all, 1)
                power_of_two(col(9), col(6), 2.0 ** -30, 2.0 ** 35)
                link(nc.vector.tensor_scalar(col(10), col(9), 2.0 ** -5, None, ALU.mult))
                nc.vector.reciprocal(col(11), col(10)).then_inc(w_scale_d, 1)
                dve.wait_ge(w_scale_d, 1)
                nc.vector.tensor_scalar(bqk[:, :], bqk[:, :], col(11), None, ALU.mult)
                link(nc.vector.tensor_scalar(bv[:, :], bv[:, :], col(11), None, ALU.mult))
                x_lo(0)
                magic(0)
                w_lo(0, wqkv_lo[:, 0, 0:2 * D], wqkv_hi[:, 0, 0:2 * D], w_stage[:, 0, 0:2 * D])
                w_lo(1, wqkv_lo[:, 1, 0:2 * D], wqkv_hi[:, 1, 0:2 * D], w_stage[:, 1, 0:2 * D])
                for k in range(2, KT):
                    w_lo(k, wqkv_lo[:, k, 0:2 * D], wqkv_hi[:, k, 0:2 * D], w_stage[:, k, 0:2 * D])
                magic(1)
                link(nc.vector.tensor_tensor(col(12), col(10), col(10), ALU.mult))
                link(nc.vector.scalar_tensor_tensor(out=col(13), in0=col(12), scalar=2.0 ** P_SHIFT, in1=col(10),
                                                    op0=ALU.mult, op1=ALU.mult))

            def w_lo(n, lo, hi, src):
                dve.wait_ge(w_hi_d, n + 1)
                nc.vector.scalar_tensor_tensor(out=lo, in0=src, scalar=col(11), in1=hi, op0=ALU.mult,
                                               op1=ALU.subtract).then_inc(w_lo_d, 1)

            def magic(n):
                dve.wait_ge(f_in[n % 3], 16 * (n // 3 + 1))
                if n >= 2:
                    dve.wait_ge(f_q_d, n - 1)
                buf = f_magic[n % 2]
                link(nc.vector.tensor_scalar(buf.bitcast(U32), f_stage[n % 3].bitcast(U32), EXPONENT, None,
                                             ALU.bitwise_and))
                nc.vector.tensor_scalar(buf, buf, E4M3_TINY, E4M3_MAGIC, ALU.max, ALU.mult).then_inc(f_magic_d, 1)

            def rounded(n):
                dve.wait_ge(f_sum_d, n + 1)
                nc.vector.tensor_tensor(piece_out(n), f_stage[n % 3], f_magic[n % 2], ALU.subtract
                                        ).then_inc(f_q_d, 1)

            def quant(n):
                rounded(n)
                if n + 2 < 12:
                    magic(n + 2)

            def scale_wout():
                dve.wait_ge(wout_max_all, 1)
                power_of_two(col(16), col(36), 2.0 ** -60, 2.0 ** 100)
                link(nc.vector.tensor_scalar(col(17), col(16), 2.0 ** -13, None, ALU.mult))
                nc.vector.tensor_tensor(col(13), col(13), col(17), ALU.mult)
                nc.vector.reciprocal(col(18), col(17)).then_inc(wout_scale_d, 1)
                dve.wait_ge(wout_scale_d, 1)

            def split_wout():
                dve.wait_ge(wout_hi_d, 1)
                nc.vector.scalar_tensor_tensor(out=wout_hl[:, 1], in0=wout_stage, scalar=col(18),
                                               in1=wout_hl[:, 0], op0=ALU.mult, op1=ALU.subtract
                                               ).then_inc(wout_lo_d, 1)

            def norms(w):
                dve.wait_ge(square_mm, 4 * w + 4)
                ins = nc.vector.tensor_reduce(col(24 + w), (b_gate, b_up)[w % 2][:, :], AX.X, ALU.max)
                if w == 1:
                    link(ins)
                    link(nc.vector.tensor_scalar(col(27, 2), col(24, 2), SQUARE_FLOOR, None, ALU.add))
                    ins = nc.vector.tensor_tensor(col(50), col(27), col(28), ALU.mult)
                ins.then_inc(norms_d, 1)

            def scale_h():
                dve.wait_ge(root_d, 1)
                link(nc.vector.reciprocal(col(52), col(51)))
                link(nc.vector.tensor_tensor(col(53), col(37), col(38), ALU.mult))
                link(nc.vector.scalar_tensor_tensor(out=col(54), in0=col(52), scalar=D / SQUARE ** 2, in1=col(53),
                                                    op0=ALU.mult, op1=ALU.mult))
                power_of_two(col(55), col(54), 2.0 ** -60, 2.0 ** 100)
                link(nc.vector.tensor_scalar(col(56), col(55), 2.0 ** -14, None, ALU.mult))
                link(nc.vector.reciprocal(col(57), col(56)))
                nc.vector.tensor_scalar(us_t[:, :], us_t[:, :], col(57), None, ALU.mult)

            def flag_down():
                dve.wait_ge(norms_d, 3)
                link(nc.vector.tensor_reduce(col(58), col(24, 3), AX.X, ALU.max))
                link(nc.vector.tensor_scalar(col(59), col(58), 0.0, None, ALU.mult))
                link(nc.vector.tensor_scalar(ds_t[:, :], ds_t[:, :], col(56), col(59), ALU.mult, ALU.add))

            def moments(ln, val, src, t):
                nc.vector.bn_stats(stats[:, ln, t], src).then_inc(bn_d[ln], 1)
                dve.wait_ge(bn_d[ln], val)
                dve.sem_inc(bn_seen, 1)
                nc.vector.bn_aggr(mv[:, ln, t], stats[:, ln, t]).then_inc(mv_d[ln], 1)

            def normalise(ln, dst, src, t):
                nc.vector.tensor_scalar(dst, src, mv[:, ln, t, 0:1], rstd[:, ln, 1, t:t + 1], ALU.subtract,
                                        ALU.mult).then_inc(nrm_d[ln], 1)

            def moments_x(n, par):
                dve.wait_ge(x_in[par], 8 * (n - par) + 16)
                for t in range(T):
                    moments(LN_X, 2 * n + t + 1, x_t[:, par, t], t)

            def normalise_x(n, par):
                dve.wait_ge(rs_d[LN_X], n + 1)
                for t in range(T):
                    normalise(LN_X, nrm[:, t], x_t[:, par, t], t)

            def x_lo(n):
                for j in range(2):
                    dve.wait_ge(x_hi_d, 2 * n + j + 1)
                    nc.vector.tensor_tensor(x_hl[:, 1, 2 * j:2 * j + 2].rearrange("p k t -> p (k t)"), b_s[j][:, :],
                                            x_hl[:, 0, 2 * j:2 * j + 2].rearrange("p k t -> p (k t)"),
                                            ALU.subtract).then_inc(x_lo_d, 1)

            def start():
                moments_x(0, 0)
                normalise_x(0, 0)
                prepare_qkv()
                quant(0)
                w_lo(KT, wqkv_lo[:, :, 2 * D:3 * D], wqkv_hi[:, :, 2 * D:3 * D], w_stage[:, :, 2 * D:3 * D])
                quant(1)
                quant(2)
                for t in range(T):
                    v_sum(0, t)
                quant(3)
                dve.wait_ge(wout_in, 32)
                dve.wait_ge(scl_in, 16 * N_SCL)
                nc.vector.tensor_reduce(col(21), gs_t[:, :], AX.X, ALU.max, apply_absolute_value=True)
                nc.vector.tensor_reduce(col(22), us_t[:, :], AX.X, ALU.max, apply_absolute_value=True)
                nc.vector.tensor_reduce(col(20), wout_stage.rearrange("p k n -> p (k n)"), AX.X, ALU.max,
                                        apply_absolute_value=True).then_inc(wout_max, 1)
                dve.wait_ge(tab_in, 16 * N_TAB)
                for c in range(T):
                    k_decay(0, c)
                masked(0, 0, 0)
                quant(4)
                scale_wout()
                masked(0, 0, 1)
                carry_and_state(0, 0, 0)
                quant(5)
                moments_x(1, 1)
                out_sum(0, 0)
                masked(0, 1, 0)
                norms(0)
                normalise_x(1, 1)
                quant(6)
                masked(0, 1, 1)
                carry_and_state(0, 1, 0)
                x_lo(1)
                quant(7)
                out_sum(0, 1)
                o_max(0, 0)
                o_max(0, 1)
                scale_o(0)
                quant(8)
                split_wout()
                o_lo(0)
                quant(9)
                norms(1)
                dve.wait_ge(square_mm, 9)
                y_moments(0, 0)
                y_moments(0, 1)
                quant(10)
                y_normalise(0, 0)
                y_normalise(0, 1)
                v_sum(1, 0)
                x1_moments(0, 0, 0)
                v_sum(1, 1)
                x1_moments(0, 0, 1)
                x1_normalise(0, 0, 0)
                quant(11)
                x1_normalise(0, 0, 1)
                scale_h()
                k_decay(1, 0)
                k_decay(1, 1)
                norms(2)

            def masked(s, c, half):
                for g in range(2 * half, 2 * half + 2):
                    dve.wait_ge(score_mm, 8 * s + 4 * c + g + 1)
                    if not (type(s) is int and s == 0 and c == 0 and g < 2):
                        dve.wait_ge(p_lo_d, 8 * s + 4 * c + g - 1)
                    nc.vector.tensor_tensor(by_head(p32[:, g % 2]), by_head(b_s[g % 2][:, :]),
                                            mask[:, heads(s, g)], ALU.mult).then_inc(p_d, 1)

            def product(v, i):
                dve.wait_ge(up_mm, 6 * v + i + 1)
                dve.wait_ge(silu_d, 6 * v + i + 1)
                if i >= 2:
                    dve.wait_ge(h_lo_d, 6 * v + i - 1)
                for j in range(2):
                    ins = nc.vector.scalar_tensor_tensor(out=h32[:, i % 2, j * TOK:(j + 1) * TOK],
                                                         in0=b_up[:, j * TOK:(j + 1) * TOK],
                                                         scalar=us_t[:, 2 * i + j:2 * i + j + 1], in1=sil[:, j],
                                                         op0=ALU.mult, op1=ALU.mult)
                ins.then_inc(h_d, 1)

            def carry_and_state(s, c, m):
                dve.wait_ge(carry_mm, 2 * s + c + 1)
                nc.vector.tensor_tensor(o32[:, c], b_t[0][:, :], decay_q[:, :], ALU.mult).then_inc(carry_d, 1)
                dve.wait_ge(state_mm, 2 * s + c + 1)
                dve.wait_ge(state_dec, 2 * s + c + 1)
                if m == per_seq - 1 and c == T - 1:
                    nc.vector.memset(state[:, :, :], 0.0).then_inc(state_u, 1)
                else:
                    for j in range(HG):
                        r = slice(DH * j, DH * (j + 1))
                        ins = nc.vector.tensor_tensor(
                            state[r, :, r], b_t[1][r, :].rearrange("p (g n) -> p g n", g=KT)[:, :, r],
                            state_d[r, :, r], ALU.add)
                    ins.then_inc(state_u, 1)

            def out_sum(s, c):
                dve.wait_ge(att_mm, 2 * s + c + 1)
                dve.wait_ge(carry_d, 2 * s + c + 1)
                for part, done in ((0, o_half_d), (1, o_d)):
                    if part:
                        dve.wait_ge(o_half_d, 2 * s + c + 1)
                    for half in range(2):
                        o = o32[:, c, half * D // 2:(half + 1) * D // 2].rearrange("p (h d) -> p h d", d=DH)
                        ins = nc.vector.tensor_tensor(o, att_out(half)[:, :, part], o, ALU.add)
                    ins.then_inc(done, 1)

            def o_max(s, c):
                dve.wait_ge(o_d, 2 * s + c + 1)
                dve.sem_inc(bn_seen, 1)
                nc.vector.tensor_reduce(o_scale[:, 0, c:c + 1], o32[:, c], AX.X, ALU.max, apply_absolute_value=True
                                        ).then_inc(o_max_d, 1)

            def scale_o(s):
                dve.wait_ge(o_max_d, 2 * s + 2)
                nc.vector.tensor_scalar(o_scale[:, 1].bitcast(U32), o_scale[:, 0].bitcast(U32), EXPONENT, None,
                                        ALU.bitwise_and).then_inc(o_exp_d, 1)
                dve.wait_ge(o_exp_d, s + 1)
                nc.vector.tensor_scalar(o_scale[:, 2], o_scale[:, 1], 2.0 ** -60, 2.0 ** -14, ALU.max, ALU.mult
                                        ).then_inc(o_div_d, 1)
                dve.wait_ge(o_div_d, s + 1)
                nc.vector.tensor_scalar(o_scale[:, 4], o_scale[:, 2], col(13), None, ALU.mult)
                nc.vector.reciprocal(o_scale[:, 3], o_scale[:, 2]).then_inc(o_mul_d, 1)
                dve.wait_ge(o_mul_d, s + 1)
                for c in range(T):
                    nc.vector.tensor_scalar(o32[:, c], o32[:, c], o_scale[:, 3, c:c + 1], None, ALU.mult
                                            ).then_inc(o_scaled_d, 1)

            def o_lo(s):
                for c in range(T):
                    dve.wait_ge(o_t_d, 2 * s + c + 1)
                    nc.vector.tensor_tensor(o_t[:, c, 1].rearrange("p k c -> p (k c)"), b_s[c][:, :],
                                            o_t[:, c, 0].rearrange("p k c -> p (k c)"), ALU.subtract
                                            ).then_inc(o_lo_d, 1)

            def v_sum(n, t):
                dve.wait_ge(v_mm, 2 * n + t + 1)
                nc.vector.tensor_tensor(v32[:, t], b_t[t][:, :], bv[:, :], ALU.add).then_inc(v_d, 1)

            def k_decay(n, c):
                dve.wait_ge(k_tr, 2 * n + c + 1)
                nc.vector.tensor_tensor(kd[:, c], b_t[c][:, :], decay_k[:, :], ALU.mult).then_inc(kd_d, 1)

            def y_moments(s, t):
                first = type(s) is int and s == 0
                dve.wait_ge(out_mm, 2 * s + t + 1)
                if not first:
                    dve.wait_ge(x1_d, 2 * s)
                nc.vector.scalar_tensor_tensor(out=y32[:, t], in0=(b_y, b_att)[t][:, :], scalar=o_scale[:, 4, t:t + 1],
                                               in1=bo[:, :], op0=ALU.mult, op1=ALU.add).then_inc(y_d, 1)
                dve.wait_ge(y_d, 2 * s + t + 1)
                moments(LN_Y, 2 * s + t + 1, y32[:, t], t)

            def y_normalise(s, t):
                dve.wait_ge(rs_d[LN_Y], 2 * s + t + 1)
                normalise(LN_Y, y32[:, t], y32[:, t], t)

            def x1_moments(s, m, t):
                dve.wait_ge(x1_d, 2 * s + t + 1)
                moments(LN_X1, 2 * s + t + 1, x1[:, m % 2, t], t)

            def x1_normalise(s, m, t):
                dve.wait_ge(rs_d[LN_X1], 2 * s + t + 1)
                normalise(LN_X1, nrm[:, t], x1[:, m % 2, t], t)

            def y2_scale(v, t):
                dve.wait_ge(down_mm, 2 * v + t + 1)
                dve.wait_ge(y2_free, v + 1)
                nc.vector.tensor_tensor(y2[:, t], (b_gate, b_up)[t][:, :], ds_t[:, :], ALU.mult
                                        ).then_inc(y2_d, 1)

            def y2_moments(v, t):
                dve.wait_ge(y2_d, 2 * v + t + 1)
                moments(LN_Y2, 2 * v + t + 1, y2[:, t], t)

            def y2_normalise(v, t):
                dve.wait_ge(rs_d[LN_Y2], 2 * v + t + 1)
                normalise(LN_Y2, y2[:, t], y2[:, t], t)

            def slot(s, m, att, nxt):
                v = s - 1
                for j in range(2):
                    dve.wait_ge(x1_hi_d, 2 * v + j + 1)
                    nc.vector.tensor_tensor(x1_hl[:, 1, 2 * j:2 * j + 2].rearrange("p k t -> p (k t)"),
                                            (b_y, b_att)[j][:, :],
                                            x1_hl[:, 0, 2 * j:2 * j + 2].rearrange("p k t -> p (k t)"),
                                            ALU.subtract).then_inc(x1_lo_d, 1)
                if att:
                    masked(s, 0, 0)
                    carry_and_state(s, 0, m)
                if early(s):
                    flag_down()
                else:
                    y2_moments(s - 2, 1)
                product(v, 0)
                if att:
                    masked(s, 0, 1)
                if not early(s):
                    y2_normalise(s - 2, 1)
                product(v, 1)
                if nxt:
                    moments_x(s + 1, (m + 1) % 2)
                product(v, 2)
                if att:
                    out_sum(s, 0)
                    masked(s, 1, 0)
                if nxt:
                    normalise_x(s + 1, (m + 1) % 2)
                product(v, 3)
                if att:
                    o_max(s, 0)
                if att:
                    masked(s, 1, 1)
                    carry_and_state(s, 1, m)
                product(v, 4)
                if nxt:
                    x_lo(s + 1)
                if nxt:
                    product(v, 5)
                if att:
                    out_sum(s, 1)
                    o_max(s, 1)
                    scale_o(s)
                if not nxt:
                    product(v, 5)
                if att:
                    o_lo(s)
                if att and not nxt:
                    for t in range(T):
                        y_moments(s, t)
                    for t in range(T):
                        y_normalise(s, t)
                    for t in range(T):
                        x1_moments(s, m, t)
                    for t in range(T):
                        x1_normalise(s, m, t)
                elif att:
                    y_moments(s, 0)
                    y_normalise(s, 0)
                    x1_moments(s, m, 0)
                    x1_normalise(s, m, 0)
                y2_scale(v, 0)
                y2_moments(v, 0)
                y2_normalise(v, 0)
                if att and nxt:
                    y_moments(s, 1)
                    y_normalise(s, 1)
                    v_sum(s + 1, 0)
                    x1_moments(s, m, 1)
                    v_sum(s + 1, 1)
                    x1_normalise(s, m, 1)
                y2_scale(v, 1)
                if nxt:
                    for c in range(T):
                        k_decay(s + 1, c)

            def end():
                y2_moments(last, 1)
                y2_normalise(last, 1)

            slots(dve.Fori, slot, start, end)


def constants():
    first = 2.0 ** (-2.0 ** (-(np.log2(H) - 3)))
    slopes = np.array([first ** (i + 1) for i in range(H)], dtype=np.float32)
    lam = np.exp(-slopes).astype(np.float64)
    pos = np.arange(P, dtype=np.float64)
    diff = pos[None, :] - pos[:, None]
    mask = np.where(diff[:, None, :] >= 0, lam[None, :, None] ** np.maximum(diff, 0.0)[:, None, :], 0.0)
    per_channel = np.repeat(lam, DH)
    rows = (lam ** P).reshape(H // HG, HG).repeat(DH, axis=1).T
    return {
        "mask_c": mask * 2.0 ** -P_SHIFT,
        "decay_q_c": per_channel[None, :] ** (pos[:, None] + 1) * 2.0 ** -P_SHIFT,
        "decay_k_c": per_channel[None, :] ** (P - 1 - pos[:, None]),
        "lam_c": np.repeat(rows[:, :, None], P, axis=2),
        "eye_c": np.eye(P),
    }


def kernel(L0_attn_x, L0_attn_w_qkv, L0_attn_b_qkv, L0_attn_w_out, L0_attn_b_out, L0_ffn_gate_w, L0_ffn_up_w,
           L0_ffn_down_w, L0_ffn_gate_scale, L0_ffn_up_scale, L0_ffn_down_scale):
    import concourse.bacc as bacc
    from concourse.bass_utils import run_bass_kernel_spmd

    def rows(a):
        return np.broadcast_to(a[None, :], (P, a.shape[0]))

    def columns(a):
        return a.reshape(-1, P).T

    x = np.asarray(L0_attn_x)
    b_qkv = np.asarray(L0_attn_b_qkv)
    laid = {
        "x": x.reshape(-1, D),
        "w_qkv_t": np.asarray(L0_attn_w_qkv).T,
        "b_qk": columns(b_qkv[:2 * D]),
        "b_v": rows(b_qkv[2 * D:]),
        "w_out_t": np.asarray(L0_attn_w_out).T,
        "b_out": rows(np.asarray(L0_attn_b_out)),
        "gate_w": np.asarray(L0_ffn_gate_w),
        "up_w": np.asarray(L0_ffn_up_w),
        "down_w": np.asarray(L0_ffn_down_w),
        "gate_s": columns(np.asarray(L0_ffn_gate_scale)),
        "up_s": columns(np.asarray(L0_ffn_up_scale)),
        "down_s": rows(np.asarray(L0_ffn_down_scale)),
    }
    laid.update({name: a.astype(np.float32) for name, a in constants().items()})
    nc = bacc.Bacc("TRN2", target_bir_lowering=False, num_devices=1)
    arrays, args = {}, {}
    for name, a in laid.items():
        a = np.ascontiguousarray(a)
        arrays[f"in_{name}"] = a
        args[name] = nc.dram_tensor(f"in_{name}", a.shape, mybir.dt.from_np(a.dtype), kind="ExternalInput").ap()
    args["out"] = nc.dram_tensor("out_x", (x.shape[0] * x.shape[1], D), F32, kind="ExternalOutput").ap()
    sandwich(nc, **args)
    r = run_bass_kernel_spmd(nc, [arrays], core_ids=[0])
    return r.results[0]["out_x"].reshape(x.shape)
```
